# Optimizing a Trainium2 kernel written in Bass

```python
import numpy as np
import jax
import jax.numpy as jnp

def _softmax(x, axis=-1):
    return jax.nn.softmax(x, axis=axis)

def _gelu(x):
    return jax.nn.gelu(x, approximate=True)

def _silu(x):
    return jax.nn.silu(x)

def _sigmoid(x):
    return jax.nn.sigmoid(x)

def _layernorm(x, axis=-1, eps=1e-05):
    m = jnp.mean(x, axis=axis, keepdims=True)
    v = jnp.var(x, axis=axis, keepdims=True)
    return (x - m) / jnp.sqrt(v + eps)

def _scatter_add(tgt, idx, src, axis=0):
    return tgt.at[idx].add(src)

def _segment_sum(src, seg, n):
    return jax.ops.segment_sum(src, seg, n)
kernel_name = 'mk_adaln_d1_jaxref_r8_6d5e88'

def setup_inputs(seed: int=0):
    np.random.seed(seed)
    _w = jnp.asarray

    def _L0_attn_setup():
        import math
        import jax, jax.numpy as jnp
        import numpy as np
        D = 128
        B, L = (4, 512)

        def _linear(x, W, b):
            return jnp.einsum('bld,ed->ble', x, W) + b

        def _ma_k_activation(x, k=0.02):
            x = x / math.sqrt(x.shape[-1])
            return jax.nn.sigmoid(x * k)

        def _ma_q_activation(x):
            x = -x / math.sqrt(x.shape[-1])
            return -jnp.where(x >= 0, x, 0.02 * x)
        key = jax.random.key(seed)
        ks = jax.random.split(key, 9)
        s = 1.0 / math.sqrt(D)
        return {'x': jax.random.normal(ks[0], (B, L, D), dtype=jnp.float32), 'Wq1': jax.random.uniform(ks[1], (D, D), jnp.float32, -s, s), 'bq1': jax.random.uniform(ks[2], (D,), jnp.float32, -s, s), 'Wk1': jax.random.uniform(ks[3], (D, D), jnp.float32, -s, s), 'bk1': jax.random.uniform(ks[4], (D,), jnp.float32, -s, s), 'Wk2': jax.random.uniform(ks[5], (D, D), jnp.float32, -s, s), 'bk2': jax.random.uniform(ks[6], (D,), jnp.float32, -s, s), 'Wproj': jax.random.uniform(ks[7], (D, D), jnp.float32, -s, s), 'bproj': jax.random.uniform(ks[8], (D,), jnp.float32, -s, s)}
    _L0_attn_in = _L0_attn_setup()

    def _L0_ffn_setup():
        import jax, jax.numpy as jnp
        import numpy as np
        E = 8
        D = 128
        F = 512
        S, B = (256, 2)
        LN_EPS = 1e-05

        def _moe_forward(input_features, centroids, ln_g, ln_b, W1, b1, W2, b2):
            s, b, d = input_features.shape
            x = jnp.swapaxes(input_features, 0, 1).reshape(-1, d)
            logits = x.astype(jnp.float32) @ centroids.astype(jnp.float32).T
            assign = jnp.argmax(logits, axis=-1)
            onehot = jax.nn.one_hot(assign, E, dtype=x.dtype)
            disp = jnp.einsum('te,td->etd', onehot, x)
            mu = disp.mean(-1, keepdims=True)
            var = disp.var(-1, keepdims=True)
            xn = (disp - mu) * jax.lax.rsqrt(var + LN_EPS)
            xn = xn * ln_g[:, None, :] + ln_b[:, None, :]
            h = jax.nn.relu(jnp.einsum('etd,edf->etf', xn, W1) + b1[:, None, :])
            y = jnp.einsum('etf,efd->etd', h, W2) + b2[:, None, :]
            y = disp + y
            out = jnp.einsum('te,etd->td', onehot, y)
            return jnp.swapaxes(out.reshape(b, s, d), 0, 1)
        key = jax.random.key(seed)
        ks = jax.random.split(key, 8)
        scale_in = 1.0 / np.sqrt(D)
        scale_ff = 1.0 / np.sqrt(F)
        return {'input_features': jax.random.normal(ks[0], (S, B, D), dtype=jnp.float32), 'centroids': jax.random.normal(ks[1], (E, D), dtype=jnp.float32) * scale_in, 'ln_g': jnp.ones((E, D), dtype=jnp.float32), 'ln_b': jnp.zeros((E, D), dtype=jnp.float32), 'W1': jax.random.normal(ks[2], (E, D, F), dtype=jnp.float32) * scale_in, 'b1': jax.random.normal(ks[3], (E, F), dtype=jnp.float32) * 0.01, 'W2': jax.random.normal(ks[4], (E, F, D), dtype=jnp.float32) * scale_ff, 'b2': jax.random.normal(ks[5], (E, D), dtype=jnp.float32) * 0.01}
    _L0_ffn_in = _L0_ffn_setup()
    _L0_c = _w((lambda *s: np.random.randn(*s).astype(np.float32) * 0.05)(32, 128))
    _L0_wmod = _w((lambda *s: np.random.randn(*s).astype(np.float32) * 0.05)(128, 6 * 128) * 128 ** (-0.5))
    _d = {'L0_attn_x': _L0_attn_in['x'], 'L0_attn_Wq1': _L0_attn_in['Wq1'], 'L0_attn_bq1': _L0_attn_in['bq1'], 'L0_attn_Wk1': _L0_attn_in['Wk1'], 'L0_attn_bk1': _L0_attn_in['bk1'], 'L0_attn_Wk2': _L0_attn_in['Wk2'], 'L0_attn_bk2': _L0_attn_in['bk2'], 'L0_attn_Wproj': _L0_attn_in['Wproj'], 'L0_attn_bproj': _L0_attn_in['bproj'], 'L0_ffn_centroids': _L0_ffn_in['centroids'], 'L0_ffn_ln_g': _L0_ffn_in['ln_g'], 'L0_ffn_ln_b': _L0_ffn_in['ln_b'], 'L0_ffn_W1': _L0_ffn_in['W1'], 'L0_ffn_b1': _L0_ffn_in['b1'], 'L0_ffn_W2': _L0_ffn_in['W2'], 'L0_ffn_b2': _L0_ffn_in['b2'], 'L0_c': _L0_c, 'L0_wmod': _L0_wmod}
    _x0 = _d['L0_attn_x']
    _d['L0_attn_x'] = jax.random.normal(jax.random.fold_in(jax.random.key(seed), 1), (32, 256, 128), dtype=_x0.dtype)
    del _x0
    return _d

def reference(L0_attn_x, L0_attn_Wq1, L0_attn_bq1, L0_attn_Wk1, L0_attn_bk1, L0_attn_Wk2, L0_attn_bk2, L0_attn_Wproj, L0_attn_bproj, L0_ffn_centroids, L0_ffn_ln_g, L0_ffn_ln_b, L0_ffn_W1, L0_ffn_b1, L0_ffn_W2, L0_ffn_b2, L0_c, L0_wmod):

    def _L0_attn_ref(x, Wq1, bq1, Wk1, bk1, Wk2, bk2, Wproj, bproj):
        import math
        import jax, jax.numpy as jnp
        import numpy as np
        D = 128
        B, L = (4, 512)

        def _linear(x, W, b):
            return jnp.einsum('bld,ed->ble', x, W) + b

        def _ma_k_activation(x, k=0.02):
            x = x / math.sqrt(x.shape[-1])
            return jax.nn.sigmoid(x * k)

        def _ma_q_activation(x):
            x = -x / math.sqrt(x.shape[-1])
            return -jnp.where(x >= 0, x, 0.02 * x)
        V = x
        K = jnp.exp(_linear(x, Wk1, bk1))
        K_cum = jnp.cumsum(K, axis=1) + 1e-06
        S = jnp.cumsum(K * V, axis=1) / K_cum
        Q = jax.nn.sigmoid(_linear(x, Wq1, bq1))
        O_ar = S * Q
        zero = jnp.zeros_like(x[:, :1, :])
        E = jnp.concatenate([zero, V[:, 1:, :] - O_ar[:, :-1, :]], axis=1)
        qk2_in = jnp.concatenate([zero, x[:, :-1, :]], axis=1)
        K2 = _ma_k_activation(_linear(qk2_in, Wk2, bk2))
        S2 = jnp.cumsum(K2 * E, axis=1)
        Q2 = _ma_q_activation(Q)
        Q2 = jnp.concatenate([zero, Q2[:, :-1, :]], axis=1)
        O_ma = S2 * Q2
        return _linear(O_ar + O_ma, Wproj, bproj)

    def _L0_ffn_ref(input_features, centroids, ln_g, ln_b, W1, b1, W2, b2):
        import jax, jax.numpy as jnp
        import numpy as np
        E = 8
        D = 128
        F = 512
        S, B = (256, 2)
        LN_EPS = 1e-05

        def _moe_forward(input_features, centroids, ln_g, ln_b, W1, b1, W2, b2):
            s, b, d = input_features.shape
            x = jnp.swapaxes(input_features, 0, 1).reshape(-1, d)
            logits = x.astype(jnp.float32) @ centroids.astype(jnp.float32).T
            assign = jnp.argmax(logits, axis=-1)
            onehot = jax.nn.one_hot(assign, E, dtype=x.dtype)
            disp = jnp.einsum('te,td->etd', onehot, x)
            mu = disp.mean(-1, keepdims=True)
            var = disp.var(-1, keepdims=True)
            xn = (disp - mu) * jax.lax.rsqrt(var + LN_EPS)
            xn = xn * ln_g[:, None, :] + ln_b[:, None, :]
            h = jax.nn.relu(jnp.einsum('etd,edf->etf', xn, W1) + b1[:, None, :])
            y = jnp.einsum('etf,efd->etd', h, W2) + b2[:, None, :]
            y = disp + y
            out = jnp.einsum('te,etd->td', onehot, y)
            return jnp.swapaxes(out.reshape(b, s, d), 0, 1)
        return _moe_forward(input_features, centroids, ln_g, ln_b, W1, b1, W2, b2)
    x = L0_attn_x
    mod = (_silu(L0_c) @ L0_wmod).reshape(L0_c.shape[0], 6, 1, -1)
    sa, ca, ga, sb, cb, gb = (mod[:, 0], mod[:, 1], mod[:, 2], mod[:, 3], mod[:, 4], mod[:, 5])
    ga = (2 * (ga >= 0) - 1) * jnp.maximum(jnp.abs(ga), 0.25)
    gb = (2 * (gb >= 0) - 1) * jnp.maximum(jnp.abs(gb), 0.25)
    h = _layernorm(x, axis=-1) * (1 + ca) + sa
    x = x + ga * _L0_attn_ref(h, L0_attn_Wq1, L0_attn_bq1, L0_attn_Wk1, L0_attn_bk1, L0_attn_Wk2, L0_attn_bk2, L0_attn_Wproj, L0_attn_bproj)
    h = _layernorm(x, axis=-1) * (1 + cb) + sb
    x = x + gb * _L0_ffn_ref(h, L0_ffn_centroids, L0_ffn_ln_g, L0_ffn_ln_b, L0_ffn_W1, L0_ffn_b1, L0_ffn_W2, L0_ffn_b2)
    return x

_drawn_inputs = setup_inputs


def setup_inputs(seed=0):
    import zlib

    import numpy as np

    out = dict(_drawn_inputs(seed))
    spreads = {'L0_ffn_ln_g': (1.0, 0.2), 'L0_ffn_ln_b': (0.0, 0.475)}
    factors = {'L0_attn_Wq1': 5.511,
     'L0_attn_bq1': 31.653,
     'L0_attn_Wk1': 3.595,
     'L0_attn_bk1': 64.0,
     'L0_attn_Wk2': 64.0,
     'L0_attn_bk2': 64.0,
     'L0_ffn_b1': 33.708,
     'L0_ffn_b2': 22.857}
    for name, (base, spread) in spreads.items():
        noise = np.random.default_rng([zlib.crc32(name.encode()), seed]).standard_normal(out[name].shape)
        drawn = base * np.exp(spread * noise) if base else spread * noise
        out[name] = jnp.asarray(drawn.astype(out[name].dtype))
    for name, factor in factors.items():
        out[name] = (out[name] * factor).astype(out[name].dtype)
    return out
```

```python
from contextlib import ExitStack

import numpy as np

import concourse.bass as bass
from concourse import mybir


P = 128
F32 = mybir.dt.float32
BF16 = mybir.dt.bfloat16
I32 = mybir.dt.int32
ALU = mybir.AluOpType
ACT = mybir.ActivationFunctionType
AX = mybir.AxisListType
LN_EPS = 1e-5
CUM_EPS = 1e-6
MA_SLOPE = 0.02
MA_K = 0.02
LN_SCALE = 2.0 ** -44
LN_SHIFT = -44 * 0.6931471805599453


def build_block(nc, x, Wq1, bq1, Wk1, bk1, Wk2, bk2, Wproj, bproj, centroids, ln_g, ln_b,
                W1, b1, W2, b2, cond, wmod, out):
    B, L, D = x.shape
    E, _, F = W1.shape
    T = B * L
    NT = T // P
    CS = 2
    CT = CS * L
    CN = CT // P
    NC = T // CT
    GT = 2 * CN
    LP = L + 1
    FT = 2 * P
    FS = FT // P
    NJ = T // FT + E - 1
    FC = F // P
    RS = T + FT
    W = D + 1
    NV = 3 + FC
    ISQ = float(D) ** -0.5
    KAPPA = MA_SLOPE * ISQ
    assert D == P and NC % 2 == 0 and B == 32

    xt = x.rearrange("b l d -> (b l) d").rearrange("(t p) d -> p t d", p=P)
    ot = out.rearrange("b l d -> (b l) d").rearrange("(t p) d -> p t d", p=P)
    W1f = W1.rearrange("e d f -> (e d) f")
    W2f = W2.rearrange("e f d -> (e f) d")
    rows_dram = nc.dram_tensor("expert_rows", ((E + 1) * RS, W), F32, kind="Internal").ap()
    x1_dram = nc.dram_tensor("x1", (T, D), F32, kind="Internal").ap()
    u_dram = nc.dram_tensor("expert_out", (T, D), F32, kind="Internal").ap()
    gates_dram = nc.dram_tensor("gates_rows", (3, B, D), F32, kind="Internal").ap()

    with ExitStack() as ctx:
        def sb(name, shape, dt=F32):
            return ctx.enter_context(nc.sbuf_tensor(name, shape, dt))

        def sem(name):
            return ctx.enter_context(nc.semaphore(name))

        ctx.enter_context(nc.allow_non_contiguous_dma(reason="biases are loaded as columns"))
        ctx.enter_context(nc.allow_low_precision(reason="numbers of slots are whole and below 2^24"))

        bank = [ctx.enter_context(nc.psum_tensor(f"bank{i}", [P, 512], F32)) for i in range(8)]
        ps_x, ps_q, ps_k, ps_k2, ps_proj, ps_z, ps_h, ps_gate = bank

        ident = sb("ident", [P, P])
        lower = sb("lower", [P, P], BF16)
        ones_bf = sb("ones_bf", [P, P], BF16)
        ones_row = sb("ones_row", [1, P])
        expert_no = sb("expert_no", [P, GT, E])
        tile_no = sb("tile_no", [P, NJ])
        part_no = sb("part_no", [P, 1])
        part_i = sb("part_i", [P, 1], I32)
        iota_i = sb("iota_i", [P, GT, E], I32)
        iota_j = sb("iota_j", [P, NJ], I32)
        token_no = sb("token_no", [P, NT], I32)
        pad_rows = sb("pad_rows", [P, FS, W])
        neg_half = sb("neg_half", [P, CN])
        seq_mask = sb("seq_mask", [P, CS * LP])
        run_mask = sb("run_mask", [P, E * (GT + 1)])
        w_raw = sb("w_raw", [P, 4, P])
        wT = sb("wT", [P, 4, P])
        bias_raw = sb("bias_raw", [P, 3])
        bias = sb("bias", [P, 3])
        cent_raw = sb("cent_raw", [E, D])
        centT = sb("centT", [P, E])
        cond_sb = sb("cond_sb", [B, D])
        cond_th = sb("cond_th", [B, D])
        cond_silu = sb("cond_silu", [B, D])
        condT = sb("condT", [P, B])
        wmod_sb = sb("wmod_sb", [P, 6 * D])
        mod = sb("mod", [P, 4, B])
        gate_raw = sb("gate_raw", [B, 2, D])
        gate_sign = sb("gate_sign", [B, 2, D])
        gate_abs = sb("gate_abs", [B, 2, D])
        gates = sb("gates", [B, 3, D])
        bproj_bc = sb("bproj_bc", [B, D])
        shared = sb("shared", [P, max(2 * B * D, NJ * FS * W)])
        wg = shared[:, 0:B * D].rearrange("p (b d) -> p b d", b=B)
        gbp_row = shared[0:1, B * D:2 * B * D].rearrange("p (b d) -> p b d", b=B)
        rows_all = shared[:, 0:NJ * FS * W].rearrange("p (j s w) -> p j s w", j=NJ, s=FS)
        gb_bc = sb("gb_bc", [P, B, D])
        lnbias = sb("lnbias", [P, 1])
        params = sb("params", [E, NV * D])

        x_in = sb("x_in", [P, 2, CN, D])
        x_res = sb("x_res", [P, 2, CN, D])
        x1_sb = sb("x1_sb", [P, 2, CN, D])
        work = sb("work", [P, 13 * 2 * CS * LP])
        used = [0]

        def carve(shape):
            a, n = used[0], int(np.prod(shape))
            used[0] += n
            names = " ".join("abcd"[:len(shape)])
            return work[:, a:a + n].rearrange(f"p ({names}) -> p {names}", **dict(zip("abcd", shape)))

        xh = sb("xh", [P, 2, CN, D])
        hT = carve([2, CS, LP])
        Kp = carve([2, CS, LP])
        KVp = carve([2, CS, LP])
        tq = carve([2, CS, LP])
        t2 = carve([2, CS, LP])
        Kc = carve([2, CS, LP])
        lnK = carve([2, CS, LP])
        SRp = carve([2, CS, LP])
        Sc = carve([2, CS, LP])
        Oar = carve([2, CS, LP])
        Ep = carve([2, CS, LP])
        S2 = carve([2, CS, LP])
        Mp = carve([2, CS, LP])
        Ot = sb("Ot", [P, 2, CS, L])
        zz = sb("zz", [P, 2, CN, D])
        h2T = sb("h2T", [P, 2, CT])
        rows = sb("rows", [P, 2, CN, W])
        bn = [sb(f"bn{i}", [P, 2, CN, 6]) for i in range(2)]
        mv = [sb(f"mv{i}", [P, 2, CN, 2]) for i in range(2)]
        veps = [sb(f"veps{i}", [P, 2, CN]) for i in range(2)]
        rstd = [sb(f"rstd{i}", [P, 2, CN]) for i in range(2)]
        negm = [sb(f"negm{i}", [P, 2, CN]) for i in range(2)]
        top = sb("top", [P, GT])
        is_top = sb("is_top", [P, GT, E])
        pick = sb("pick", [P, GT])
        pick_c = sb("pick_c", [P, GT])
        onehot = sb("onehot", [P, GT, E], BF16)
        run_in = sb("run_in", [P, E, GT + 1])
        run_out = sb("run_out", [P, E, GT + 1])
        slot_f = sb("slot_f", [P, E, GT])
        slot_m = sb("slot_m", [P, E, GT])
        slots = sb("slots", [P, GT], I32)
        count_f = sb("count_f", [P, E])
        region = sb("region", [P, E + 1])
        count_i = sb("count_i", [P, E], I32)
        end_i = sb("end_i", [P, E], I32)
        tiles_i = sb("tiles_i", [P, E], I32)
        tiles_f = sb("tiles_f", [P, E])
        tiles_end = sb("tiles_end", [P, E])
        shift = sb("shift", [P, E + 1])
        past = sb("past", [P, NJ, E])
        tile_e = sb("tile_e", [P, NJ])
        tile_ec = sb("tile_ec", [P, NJ])
        is_e = sb("is_e", [P, NJ, E + 1])
        row_f = sb("row_f", [P, NJ])
        row_g = sb("row_g", [P, NJ])
        plan = sb("plan", [P, NJ, 2], I32)
        sel = sb("sel", [E, NJ])
        par = sb("par", [P, NV, NJ])
        used[0] = 0
        mail = sb("mail", [1, 2, 2], I32)
        w1_sb = carve([2, F])
        w2_sb = carve([2, FC, D])
        bbn = sb("bbn", [P, 2, FS, 6])
        bmv = sb("bmv", [P, 2, FS, 2])
        bveps = sb("bveps", [P, 2, FS])
        brstd = sb("brstd", [P, 2, FS])
        bz = carve([2, FS, D])
        zT = carve([2, FT])
        hid = carve([2, FC, FT])
        yT = carve([2, FT])
        u_sb = carve([2, FS, D])
        ids = sb("ids", [P, 2, FS], I32)
        uc = carve([4, GT, D])
        x1c = sb("x1c", [P, 4, GT, D])

        s_w = sem("weights_in"); s_small = sem("small_in"); s_mod_in = sem("mod_in")
        s_x = [sem(f"x_in{i}") for i in range(2)]
        s_xr = [sem(f"x_res{i}") for i in range(2)]
        s_x1out = [sem(f"x1_out{i}") for i in range(2)]
        s_const = sem("constants"); s_ident = sem("ident_ready"); s_iota = sem("iota_ready")
        s_pads = sem("pads_ready"); s_zero = sem("leading_columns")
        s_setup_pe = sem("setup_pe"); s_setup_act = sem("setup_act"); s_modw = sem("mod_ready"); s_lnb = sem("ln_shift_ready")
        s_th = sem("cond_tanh"); s_silu = sem("cond_silu"); s_gate = sem("gate_steps"); s_gabs = sem("gate_abs"); s_ise = sem("is_expert"); s_tok = sem("token_numbers")
        s_gout = sem("gates_out"); s_gin = sem("gates_in"); s_gbin = sem("gb_in"); s_wg = sem("wg_ready")
        names = ("bn aggr veps rstd negm norm").split()
        sA = {n: sem("x_" + n) for n in names}
        sB = {n: sem("z_" + n) for n in names}
        s_xT = sem("xT_psum"); s_hT = sem("hT_ready"); s_qkv = sem("qkv_psum")
        s_tq = sem("tq_ready"); s_t2 = sem("t2_ready"); s_K = sem("K_ready"); s_KV = sem("KV_ready")
        s_Kc = sem("Kc_ready"); s_Sc = sem("Sc_ready"); s_ln = sem("lnK_ready"); s_R = sem("R_ready")
        s_SR = sem("SR_ready"); s_Oar = sem("Oar_ready"); s_E = sem("E_ready"); s_KE = sem("KE_ready")
        s_S2 = sem("S2_ready"); s_M = sem("M_ready"); s_O = sem("O_ready")
        s_proj = sem("proj_psum"); s_x1 = sem("x1_ready")
        s_zT = sem("zT_psum"); s_h2T = sem("h2T_ready"); s_h2 = sem("h2_psum"); s_row = sem("rows_ready")
        s_gates = sem("logits_psum"); s_oh = sem("onehot_steps"); s_ohr = sem("onehot_ready")
        s_rank = sem("rank_psum"); s_run = sem("run_steps"); s_slot = sem("slots_ready")
        s_scat = [sem(f"rows_scattered{i}") for i in range(2)]
        s_plan = sem("plan_steps"); s_planned = sem("plan_ready"); s_sel = sem("params_psum")
        s_par = sem("params_ready"); s_count = sem("counts_ready"); s_pad_out = sem("pads_out")
        s_mail = sem("mail_ready"); s_read = sem("mail_read")
        s_rin = [sem(f"rows_in{i}") for i in range(2)]
        s_win = [sem(f"expert_in{i}") for i in range(2)]
        b_bn = sem("b_bn"); b_aggr = sem("b_aggr"); b_veps = sem("b_veps"); b_rstd = sem("b_rstd")
        b_z = sem("b_z"); b_zTp = sem("b_zT_psum"); b_zT = sem("b_zT_ready")
        b_l1 = [sem(f"b_hidden_psum{i}") for i in range(2)]
        b_hidA = sem("b_hidden_act"); b_hidD = sem("b_hidden_dve")
        b_y = sem("b_y_psum"); b_yT = sem("b_yT_ready"); b_up = sem("b_u_psum"); b_u = sem("b_u_ready")
        b_ids = sem("b_ids_ready")
        s_uout = [sem(f"u_out{i}") for i in range(2)]
        s_uin = [sem(f"u_in{i}") for i in range(4)]
        c_mul = sem("c_mul"); c_add = sem("c_add")
        s_out = [sem(f"out_done{i}") for i in range(4)]

        def alone(eng):
            eng.sem_inc(s_met[eng], 1)

        def wait(eng, s, value):
            if isinstance(value, int) and value <= 0:
                return
            eng.wait_ge(s, value)

        class At:

            def __init__(self, c, half, par):
                self.c, self.half, self.par = c, half, par
                self.fixed = isinstance(c, int)

            def __add__(self, o):
                k = self.par + o
                return At(self.c + o, self.half + k // 2, k % 2)

            def within(self, n):
                return not self.fixed or 0 <= self.c < n

        def walk(eng, first, lo, hi, last, body):
            for c in range(first, lo):
                body(At(c, c // 2, c % 2))
            with eng.Fori(lo // 2, hi // 2) as i:
                body(At(i * 2, i, 0))
                body(At(i * 2 + 1, i, 1))
            for c in range(hi, last):
                body(At(c, c // 2, c % 2))

        A_SPAN = (-2, 6, 14, NC + 4)
        B_SPAN = (-3, 4, 36, NJ + 2)

        s_met = {eng: sem(f"met_{n}") for n, eng in (("pool", nc.gpsimd), ("dve", nc.vector), ("sp", nc.sync))}
        block = ctx.enter_context(nc.Block())

        @block.sync
        def _(sp):
            for n, w in enumerate((Wq1, Wk1, Wk2, Wproj)):
                sp.dma_start(w_raw[:, n, :], w).then_inc(s_w, 16)
            for k in range(2):
                sp.dma_start(x_in[:, k, :, :], xt[:, k * CN:(k + 1) * CN, :]).then_inc(s_x[k], 16)
            sp.wait_ge(s_gate, 6)
            sp.dma_start(gates_dram.rearrange("g b d -> b g d"), gates[:, :, :]).then_inc(s_gout, 16)
            sp.wait_ge(s_gout, 16)
            sp.dma_start(wg[:, :, :].rearrange("p b d -> p (b d)"),
                         gates_dram[0].rearrange("b d -> (b d)").partition_broadcast(P)).then_inc(s_gin, 16)
            sp.dma_start(gbp_row[:, :, :].rearrange("o b d -> o (b d)"),
                         gates_dram[2].rearrange("b d -> (b d)").partition_broadcast(1)).then_inc(s_gin, 16)

            x1t = x1_dram.rearrange("(t p) d -> p t d", p=P)

            def stream(c):
                m = c + 2
                if m.within(NC) and not (m.fixed and m.c < 2):
                    wait(sp, sA["norm"], CN * (m.c - 1))
                    alone(sp)
                    wait(sp, s_x[m.par], 16 * m.half)
                    alone(sp)
                    sp.dma_start(x_in[:, m.par, :, :], xt[:, bass.ds(m.c * CN, CN), :]).then_inc(s_x[m.par], 16)
                if c.within(NC):
                    wait(sp, s_x1, c.c - 1)
                    alone(sp)
                    wait(sp, s_xr[c.par], 16 * c.half)
                    alone(sp)
                    sp.dma_start(x_res[:, c.par, :, :], xt[:, bass.ds(c.c * CN, CN), :]).then_inc(s_xr[c.par], 16)
                o = c + (-1)
                if o.within(NC):
                    wait(sp, s_x1, o.c + 1)
                    alone(sp)
                    wait(sp, s_x1out[o.par], 16 * o.half)
                    alone(sp)
                    sp.dma_start(x1t[:, bass.ds(o.c * CN, CN), :], x1_sb[:, o.par, :, :]
                                 ).then_inc(s_x1out[o.par], 16)

            walk(sp, 0, 4, 14, NC + 1, stream)
            sp.dma_start(gb_bc[:, :, :].rearrange("p b d -> p (b d)"),
                         gates_dram[1].rearrange("b d -> (b d)").partition_broadcast(P)).then_inc(s_gbin, 16)

            sp.wait_ge(s_pads, 2)
            sp.dma_start(rows_dram[E * RS:E * RS + FT, :].rearrange("(s p) w -> p s w", p=P),
                         pad_rows[:, :, :]).then_inc(s_pad_out, 16)
            sp.wait_ge(s_count, 1)
            for e in range(E):
                end = sp.value_load(end_i[0:1, e:e + 1], min_val=e * RS, max_val=e * RS + T)
                sp.dma_start(rows_dram[bass.ds(end, FT), :].rearrange("(s p) w -> p s w", p=P),
                             pad_rows[:, :, :]).then_inc(s_pad_out, 16)
            sp.wait_ge(s_pad_out, 16 * (E + 1))
            for k in range(2):
                sp.wait_ge(s_scat[k], 16 * NT // 2)

            def load_tile(j):
                sp.wait_ge(s_mail, j.c + 1)
                alone(sp)
                r = sp.value_load(mail[0:1, j.par, 1:2], min_val=0, max_val=E * RS)
                sp.sem_inc(s_read, 1)
                alone(sp)
                wait(sp, s_rin[j.par], 16 * j.half)
                alone(sp)
                sp.dma_start(rows_all[:, bass.ds(j.c, 1), :, :].rearrange("p j s w -> p (j s) w"),
                             rows_dram[bass.ds(r, FT), :].rearrange("(s p) w -> p s w", p=P)
                             ).then_inc(s_rin[j.par], 16)

            walk(sp, 0, 2, 38, NJ, load_tile)

            for k in range(2):
                sp.wait_ge(s_uout[k], 16 * FS * ((NJ + 1 - k) // 2))
                sp.wait_ge(s_x1out[k], 16 * NC // 2)
            ut = u_dram.rearrange("(t p) d -> p t d", p=P)
            for g in range(NT // GT):
                if g >= 4:
                    sp.wait_ge(s_out[g % 4], 16 * (g // 4))
                sp.dma_start(uc[:, g % 4, :, :], ut[:, g * GT:(g + 1) * GT, :]).then_inc(s_uin[g % 4], 16)
                sp.dma_start(x1c[:, g % 4, :, :], x1t[:, g * GT:(g + 1) * GT, :]).then_inc(s_uin[g % 4], 16)

        @block.gpsimd
        def _(pool):
            pool.memset(ident[:, :], 0.0).then_inc(s_ident, 1)
            pool.wait_ge(s_ident, 1)
            pool.affine_select(out=ident[:, :], in_=ident[:, :], compare_op=ALU.not_equal, fill=1.0,
                               base=0, pattern=[[-1, P]], channel_multiplier=1).then_inc(s_ident, 1)
            pool.memset(neg_half[:, :], -0.5).then_inc(s_const, 1)
            pool.memset(ones_row[:, :], 1.0).then_inc(s_const, 1)
            pool.memset(ones_bf[:, :], 1.0).then_inc(s_const, 1)
            pool.memset(lower[:, :], 1.0).then_inc(s_const, 1)
            pool.wait_ge(s_const, 4)
            pool.affine_select(out=lower[:, :], in_=lower[:, :], compare_op=ALU.is_gt, fill=0.0,
                               base=0, pattern=[[1, P]], channel_multiplier=-1).then_inc(s_const, 1)

            def rsqrt_steps(at, s, mv_t, veps_t, rstd_t, negm_t, src, dst):
                k = at.par
                wait(pool, s["aggr"], CN * (at.c + 1))
                alone(pool)
                pool.tensor_scalar(veps_t[:, k, :], mv_t[:, k, :, 1], LN_EPS, None, ALU.add).then_inc(s["veps"], 1)
                pool.tensor_scalar(negm_t[:, k, :], mv_t[:, k, :, 0], -1.0, None, ALU.mult).then_inc(s["negm"], 1)
                wait(pool, s["veps"], at.c + 1)
                pool.tensor_tensor(rstd_t[:, k, :], veps_t[:, k, :], neg_half[:, :], ALU.pow).then_inc(s["rstd"], 1)
                wait(pool, s["negm"], at.c + 1)
                wait(pool, s["rstd"], at.c + 1)
                alone(pool)
                for t in range(CN):
                    pool.tensor_scalar(dst[:, k, t, :], src(t), negm_t[:, k, t:t + 1], rstd_t[:, k, t:t + 1],
                                       ALU.add, ALU.mult).then_inc(s["norm"], 1)

            def scatter(c, g, first):
                wait(pool, s_scat[first], 16 * CN * g)
                alone(pool)
                pool.tensor_copy(rows[:, first, :, D:W].bitcast(I32),
                                 token_no[:, bass.ds(c * CN, CN)].unsqueeze(2)).then_inc(s_tok, 1)
                wait(pool, s_tok, c + 1)
                wait(pool, s_row, c + 1)
                wait(pool, s_slot, g + 1)
                alone(pool)
                for t in range(CN):
                    pool.indirect_dma_start(rows_dram, bass.IndirectOffsetOnAxis(
                        ap=slots[:, first * CN + t:first * CN + t + 1], axis=0),
                        rows[:, first, t, :], None).then_inc(s_scat[first], 16)

            def front_and_back(c):
                if c.within(NC):
                    k = c.par
                    wait(pool, s_R, c.c + 1)
                    wait(pool, s_Sc, c.c + 1)
                    pool.tensor_tensor(SRp[:, k, :, 1:LP], Sc[:, k, :, 1:LP], lnK[:, k, :, 1:LP],
                                       ALU.mult).then_inc(s_SR, 1)
                s = c + (-4)
                if s.within(NC):
                    if s.fixed and s.c == 0:
                        pool.wait_ge(s_iota, 1)
                    scatter(s.c, s.half, s.par)
                z = c + (-1)
                if z.within(NC):
                    wait(pool, s_zT, z.c - 1)
                    rsqrt_steps(z, sB, mv[1], veps[1], rstd[1], negm[1],
                                lambda t: x1_sb[:, z.par, t, :], zz)
                a = c + 2
                if a.within(NC):
                    wait(pool, s_xT, a.c - 1)
                    rsqrt_steps(a, sA, mv[0], veps[0], rstd[0], negm[0],
                                lambda t: x_in[:, a.par, t, :], xh)
                n = c + 1
                if n.within(NC):
                    k = n.par
                    wait(pool, s_hT, 2 * (n.c + 1))
                    wait(pool, s_K, n.c + 1)
                    wait(pool, s_zero, 6)
                    pool.tensor_tensor(KVp[:, k, :, 1:LP], Kp[:, k, :, 1:LP], hT[:, k, :, 1:LP],
                                       ALU.mult).then_inc(s_KV, 1)

            front_and_back(At(-2, -1, 0))
            pool.iota(token_no[:, :], pattern=[[P, NT]], base=0, channel_multiplier=1).then_inc(s_iota, 1)
            pool.iota(iota_i[:, :, :], pattern=[[0, GT], [1, E]], base=-E, channel_multiplier=0).then_inc(s_iota, 1)
            pool.iota(iota_j[:, :], pattern=[[1, NJ]], base=0, channel_multiplier=0).then_inc(s_iota, 1)
            pool.iota(part_i[:, :], pattern=[[0, 1]], base=0, channel_multiplier=1).then_inc(s_iota, 1)
            pool.memset(pad_rows[:, :, :], 0.0).then_inc(s_pads, 1)
            pool.wait_ge(s_pads, 1)
            pool.memset(pad_rows[:, :, D:W].bitcast(I32), T).then_inc(s_pads, 1)
            pool.memset(run_mask[:, :], 1.0).then_inc(s_iota, 1)
            pool.wait_ge(s_iota, 5)
            pool.tensor_copy(expert_no[:, :, :], iota_i[:, :, :]).then_inc(s_iota, 1)
            pool.tensor_copy(tile_no[:, :], iota_j[:, :]).then_inc(s_iota, 1)
            pool.tensor_copy(part_no[:, :], part_i[:, :]).then_inc(s_iota, 1)
            pool.memset(run_mask[:, :].rearrange("p (e t) -> p e t", e=E)[:, :, 0:1], 0.0).then_inc(s_iota, 1)
            for e in range(E):
                pool.memset(run_out[:, e, GT:GT + 1], float(e * RS)).then_inc(s_iota, 1)
            for e in range(E + 1):
                pool.memset(region[:, e:e + 1], float(e * RS)).then_inc(s_iota, 1)
            walk(pool, *(-1,) + A_SPAN[1:], front_and_back)

            def expert_step(j):
                m = j + 3
                if m.within(NJ):
                    if m.fixed and m.c == 0:
                        pool.wait_ge(s_planned, 2)
                    wait(pool, s_read, m.c - 1)
                    alone(pool)
                    pool.tensor_copy(mail[0:1, m.par, :],
                                     plan[0:1, bass.ds(m.c, 1), :].rearrange("p o w -> p (o w)")
                                     ).then_inc(s_mail, 1)
                n = j + 2
                if n.within(NJ):
                    k = n.par
                    wait(pool, b_aggr, FS * (n.c + 1))
                    alone(pool)
                    pool.tensor_scalar(bveps[:, k, :], bmv[:, k, :, 1], LN_EPS, None, ALU.add).then_inc(b_veps, 1)
                    wait(pool, b_veps, n.c + 1)
                    wait(pool, b_z, FS * (n.c - 1))
                    pool.tensor_tensor(brstd[:, k, :], bveps[:, k, :], neg_half[:, 0:FS], ALU.pow).then_inc(b_rstd, 1)
                u = j + (-1)
                if u.within(NJ):
                    k = u.par
                    wait(pool, s_uout[k], 16 * FS * u.half)
                    alone(pool)
                    pool.tensor_copy(ids[:, k, :], rows_all[:, bass.ds(u.c, 1), :, D:W].bitcast(I32)
                                     .rearrange("p j s w -> p (j s w)")).then_inc(b_ids, 1)
                    wait(pool, b_ids, u.c + 1)
                    wait(pool, b_u, u.c + 1)
                    alone(pool)
                    for t in range(FS):
                        pool.indirect_dma_start(u_dram, bass.IndirectOffsetOnAxis(ap=ids[:, k, t:t + 1], axis=0),
                                                u_sb[:, k, t, :], None, bounds_check=T - 1,
                                                oob_is_err=False).then_inc(s_uout[k], 16)

            walk(pool, *B_SPAN, expert_step)

        @block.tensor
        def _(pe):
            pe.wait_ge(s_ident, 2)
            pe.wait_ge(s_w, 64)
            for n in range(4):
                pe.transpose(ps_q[:, n * P:(n + 1) * P], w_raw[:, n, :], ident[:, :]).then_inc(s_setup_pe, 1)
            pe.wait_ge(s_silu, 1)
            pe.transpose(ps_k[:, 0:B], cond_silu[:, :], ident[0:B, 0:B])
            pe.transpose(ps_k[:, B:B + E], cent_raw[:, :], ident[0:E, 0:E]).then_inc(s_setup_pe, 1)
            pe.wait_ge(s_setup_act, 2)
            pe.wait_ge(s_mod_in, 16)
            for n, part in enumerate((0, 1, 3, 4)):
                mm = pe.matmul(ps_k2[:, n * B:(n + 1) * B], wmod_sb[:, part * D:(part + 1) * D], condT[:, :],
                               start=True, stop=True)
            mm.then_inc(s_setup_pe, 1)
            for n, part in enumerate((2, 5)):
                mm = pe.matmul(ps_proj[0:B, n * D:(n + 1) * D], condT[:, :], wmod_sb[:, part * D:(part + 1) * D],
                               start=True, stop=True)
            mm.then_inc(s_setup_pe, 1)
            pe.wait_ge(s_setup_act, 3)
            pe.wait_ge(s_modw, 4)
            pe.wait_ge(s_gate, 1)

            def ranks(g):
                wait(pe, s_ohr, g + 1)
                oh = onehot[:, :, :].rearrange("p t e -> p e t")
                pe.matmul(ps_gate[:, GT * E:2 * GT * E].rearrange("p (e t) -> p e t", e=E), lower[:, :], oh,
                          start=True, stop=True)
                pe.matmul(ps_gate[:, 2 * GT * E:3 * GT * E].rearrange("p (e t) -> p e t", e=E), ones_bf[:, :], oh,
                          start=True, stop=True).then_inc(s_rank, 1)

            def chunk(c):
                if c.par == 0:
                    g = c + (-4)
                    if g.within(NC):
                        if g.fixed and g.c == 0:
                            pe.wait_ge(s_const, 5)
                        ranks(g.half)
                o = c + (-1)
                if o.within(NC):
                    if o.fixed and o.c == 0:
                        pe.wait_ge(s_wg, 1)
                        pe.wait_ge(s_gin, 32)
                    wait(pe, s_O, o.c + 1)
                    wait(pe, s_x1, o.c)
                    for t in range(CN):
                        s = t * P // L
                        seq = o.c * CS + s
                        dst = ps_proj[:, t * P:(t + 1) * P]
                        pe.matmul(dst, Ot[:, o.par, s, (t * P) % L:(t * P) % L + P],
                                  wg[:, bass.ds(seq, 1), :].rearrange("p o d -> p (o d)"), start=True, stop=False)
                        mm = pe.matmul(dst, ones_row[:, :],
                                       gbp_row[:, bass.ds(seq, 1), :].rearrange("p o d -> p (o d)"),
                                       start=False, stop=True)
                    mm.then_inc(s_proj, 1)
                n = c + 1
                if n.within(NC):
                    k = n.par
                    wait(pe, sA["norm"], CN * (n.c + 1))
                    wait(pe, s_hT, 2 * n.c)
                    for t in range(CN):
                        mm = pe.transpose(ps_x[:, t * P:(t + 1) * P], xh[:, k, t, :], ident[:, :])
                    mm.then_inc(s_xT, 1)
                z = c + (-2)
                if z.within(NC):
                    k = z.par
                    wait(pe, sB["norm"], CN * (z.c + 1))
                    wait(pe, s_h2T, 2 * z.c)
                    for t in range(CN):
                        mm = pe.transpose(ps_z[:, t * P:(t + 1) * P], zz[:, k, t, :], ident[:, :])
                    mm.then_inc(s_zT, 1)
                if n.within(NC):
                    k = n.par
                    wait(pe, s_hT, 2 * (n.c + 1))
                    for m, (dst, free) in enumerate(((ps_q, s_tq), (ps_k2, s_t2), (ps_k, s_K))):
                        wait(pe, free, n.c)
                        pe.matmul(dst[:, :], wT[:, (0, 2, 1)[m], :], hT[:, k, :, 1:LP],
                                  start=True, stop=True).then_inc(s_qkv, 1)
                if z.within(NC):
                    k = z.par
                    wait(pe, s_h2T, 2 * (z.c + 1))
                    wait(pe, s_row, z.c)
                    for t in range(CN):
                        mm = pe.transpose(ps_h[:, t * P:(t + 1) * P], h2T[:, k, t * P:(t + 1) * P], ident[:, :])
                    mm.then_inc(s_h2, 1)
                    if k == 0:
                        wait(pe, s_slot, z.half)
                    for t in range(CN):
                        at = (k * CN + t) * E
                        mm = pe.matmul(ps_gate[:, at:at + E], h2T[:, k, t * P:(t + 1) * P], centT[:, :],
                                       start=True, stop=True)
                    mm.then_inc(s_gates, 1)

            walk(pe, *A_SPAN, chunk)

            pe.wait_ge(s_planned, 1)
            pe.wait_ge(s_small, 16 * 10)
            for n in range(NV):
                mm = pe.matmul(ps_x[:, n * NJ:(n + 1) * NJ], params[:, n * D:(n + 1) * D], sel[:, :],
                               start=True, stop=True)
            mm.then_inc(s_sel, 1)

            for s in (s_x1, s_row, s_K, s_tq, s_t2):
                pe.wait_ge(s, NC)
            pe.wait_ge(s_h2T, 2 * NC)

            def expert_tile(j):
                if j.within(NJ):
                    k = j.par
                    wait(pe, b_zT, j.c + 1)
                    wait(pe, s_win[k], 32 * (j.half + 1))
                    if j.fixed and j.c == 0:
                        pe.wait_ge(s_par, 1)
                    for f in range(FC):
                        if f == 0:
                            wait(pe, b_hidA, j.c)
                        if f == 2:
                            wait(pe, b_hidD, j.c)
                        mm = pe.matmul((ps_proj, ps_h)[f // 2][:, (f % 2) * FT:(f % 2 + 1) * FT],
                                       w1_sb[:, k, f * P:(f + 1) * P], zT[:, k, :], start=True, stop=True)
                        if f % 2:
                            mm.then_inc(b_l1[f // 2], 1)
                n = j + 1
                if n.within(NJ):
                    wait(pe, b_z, FS * (n.c + 1))
                    wait(pe, b_zT, n.c)
                    for t in range(FS):
                        mm = pe.transpose(ps_z[:, t * P:(t + 1) * P], bz[:, n.par, t, :], ident[:, :])
                    mm.then_inc(b_zTp, 1)
                u = j + (-1)
                if u.within(NJ):
                    wait(pe, b_yT, u.c + 1)
                    wait(pe, b_u, u.c)
                    for t in range(FS):
                        mm = pe.transpose(ps_k2[:, t * P:(t + 1) * P], yT[:, u.par, t * P:(t + 1) * P], ident[:, :])
                    mm.then_inc(b_up, 1)
                if j.within(NJ):
                    k = j.par
                    for f in range(FC):
                        if f == 0:
                            wait(pe, b_hidA, j.c + 1)
                        if f == 2:
                            wait(pe, b_hidD, j.c + 1)
                        mm = pe.matmul((ps_q, ps_k)[k][:, 0:FT], w2_sb[:, k, f, :], hid[:, k, f, :],
                                       start=(f == 0), stop=(f == FC - 1))
                    mm.then_inc(b_y, 1)

            walk(pe, *B_SPAN, expert_tile)

        @block.scalar
        def _(act):
            act.dma_start(cond_sb[:, :], cond).then_inc(s_small, 16)
            act.dma_start(cent_raw[:, :], centroids).then_inc(s_small, 16)
            for n, v in enumerate((bq1, bk2, bk1)):
                act.dma_start(bias_raw[:, n:n + 1], v.rearrange("(p o) -> p o", o=1)).then_inc(s_small, 16)
            act.dma_start(wmod_sb[:, :], wmod).then_inc(s_mod_in, 16)
            act.dma_start(bproj_bc[:, :], bproj.partition_broadcast(B)).then_inc(s_small, 16)
            act.dma_start(params[:, 0:D], ln_g).then_inc(s_small, 16)
            act.dma_start(params[:, D:2 * D], ln_b).then_inc(s_small, 16)
            act.dma_start(params[:, 2 * D:3 * D], b2).then_inc(s_small, 16)
            act.dma_start(params[:, 3 * D:NV * D], b1).then_inc(s_small, 16)
            act.wait_ge(s_small, 16 * 10)
            act.activation(cond_th[:, :], cond_sb[:, :], ACT.Tanh, scale=0.5).then_inc(s_th, 1)
            act.wait_ge(s_setup_pe, 4)
            act.activation(wT[:, :, :], ps_q[:, :].rearrange("p (n d) -> p n d", n=4), ACT.Copy).then_inc(s_setup_act, 1)
            act.wait_ge(s_setup_pe, 5)
            act.activation(condT[:, :], ps_k[:, 0:B], ACT.Copy, scale=0.5).then_inc(s_setup_act, 1)
            act.activation(centT[:, :], ps_k[:, B:B + E], ACT.Copy).then_inc(s_setup_act, 1)
            act.mul(bias[:, 0:1], bias_raw[:, 0:1], 0.5).then_inc(s_setup_act, 1)
            act.mul(bias[:, 1:2], bias_raw[:, 1:2], 0.5 * MA_K * ISQ).then_inc(s_setup_act, 1)
            act.copy(bias[:, 2:3], bias_raw[:, 2:3]).then_inc(s_setup_act, 1)
            act.wait_ge(s_setup_act, 6)

            def chunk(c):
                n = c + 1
                if n.within(NC):
                    if n.fixed and n.c == 0:
                        act.wait_ge(s_modw, 4)
                    wait(act, s_xT, n.c + 1)
                    wait(act, s_O, n.c - 1)
                    for s in range(CS):
                        act.activation(hT[:, n.par, s, 1:LP], ps_x[:, s * L:(s + 1) * L], ACT.Identity,
                                       bias=mod[:, 0, bass.ds(n.c * CS + s, 1)],
                                       scale=mod[:, 1, bass.ds(n.c * CS + s, 1)]).then_inc(s_hT, 1)
                if c.within(NC):
                    k = c.par
                    if c.fixed and c.c == 0:
                        act.wait_ge(s_lnb, 1)
                    wait(act, s_Kc, c.c + 1)
                    act.activation(lnK[:, k, :, :], Kc[:, k, :, :], ACT.Ln, scale=LN_SCALE).then_inc(s_ln, 1)
                    wait(act, s_ln, c.c + 1)
                    act.activation(lnK[:, k, :, :], lnK[:, k, :, :], ACT.Exp, scale=-1.0,
                                   bias=lnbias[:, :]).then_inc(s_R, 1)
                z = c + (-2)
                if z.within(NC):
                    k = z.par
                    wait(act, s_zT, z.c + 1)
                    wait(act, s_gates, z.c - 1)
                    for s in range(CS):
                        act.activation(h2T[:, k, s * L:(s + 1) * L], ps_z[:, s * L:(s + 1) * L], ACT.Identity,
                                       bias=mod[:, 2, bass.ds(z.c * CS + s, 1)],
                                       scale=mod[:, 3, bass.ds(z.c * CS + s, 1)]).then_inc(s_h2T, 1)
                if n.within(NC):
                    k = n.par
                    for m, (src, dst, f, scale, done) in enumerate((
                            (ps_q, tq, ACT.Tanh, 0.5, s_tq), (ps_k2, t2, ACT.Tanh, 0.5 * MA_K * ISQ, s_t2),
                            (ps_k, Kp, ACT.Exp, 1.0, s_K))):
                        wait(act, s_qkv, 3 * n.c + m + 1)
                        if n.fixed and n.c == 0 and m == 2:
                            act.wait_ge(s_zero, 6)
                        act.activation(dst[:, k, :, 1:LP], src[:, :].rearrange("p (s l) -> p s l", s=CS), f,
                                       bias=bias[:, m:m + 1], scale=scale).then_inc(done, 1)
                if z.within(NC):
                    k = z.par
                    wait(act, s_h2, z.c + 1)
                    wait(act, s_scat[k], 16 * CN * z.half)
                    act.activation(rows[:, k, :, 0:D], ps_h[:, :].rearrange("p (t d) -> p t d", t=CN),
                                   ACT.Copy).then_inc(s_row, 1)

            walk(act, *A_SPAN, chunk)

            act.wait_ge(s_sel, 1)
            act.activation(par[:, :, :], ps_x[:, 0:NV * NJ].rearrange("p (v j) -> p v j", v=NV),
                           ACT.Copy).then_inc(s_par, 1)
            act.wait_ge(s_par, 1)

            def column(v, j):
                return par[:, v, bass.ds(j, 1)]

            act.wait_ge(s_planned, 2)

            def expert_tile(j):
                n = j + 1
                if n.within(NJ):
                    e = act.value_load(plan[0:1, bass.ds(n.c, 1), 0:1].rearrange("p o w -> p (o w)"),
                                       min_val=0, max_val=E - 1)
                    wait(act, b_y, n.c - 1)
                    act.dma_start(w1_sb[:, n.par, :], W1f[bass.ds(e * D, D), :]).then_inc(s_win[n.par], 16)
                    act.dma_start(w2_sb[:, n.par, :, :],
                                  W2f[bass.ds(e * F, F), :].rearrange("(k p) d -> p k d", p=P)
                                  ).then_inc(s_win[n.par], 16)
                if j.within(NJ):
                    k = j.par
                    wait(act, b_l1[0], j.c + 1)
                    wait(act, b_y, j.c - 1)
                    for f in range(2):
                        a = act.activation(hid[:, k, f, :], ps_proj[:, f * FT:(f + 1) * FT], ACT.Relu,
                                           bias=column(3 + f, j.c))
                    a.then_inc(b_hidA, 1)
                n = j + 1
                if n.within(NJ):
                    wait(act, b_zTp, n.c + 1)
                    wait(act, b_l1[1], n.c - 1)
                    act.activation(zT[:, n.par, :], ps_z[:, 0:FT], ACT.Identity, bias=column(1, n.c),
                                   scale=column(0, n.c)).then_inc(b_zT, 1)
                if j.within(NJ):
                    wait(act, b_y, j.c + 1)
                    wait(act, b_up, j.c - 1)
                    act.activation(yT[:, k, :], (ps_q, ps_k)[k][:, 0:FT], ACT.Identity,
                                   bias=column(2, j.c)).then_inc(b_yT, 1)

            walk(act, *B_SPAN, expert_tile)

            for g in range(NT // GT):
                act.wait_ge(c_add, g + 1)
                act.dma_start(ot[:, g * GT:(g + 1) * GT, :], x1c[:, g % 4, :, :]).then_inc(s_out[g % 4], 16)
            for k in range(4):
                act.wait_ge(s_out[k], 16 * NT // GT // 4)

        @block.vector
        def _(dve):
            dve.memset(seq_mask[:, :], 1.0).then_inc(s_zero, 1)
            for k, (buf, v) in enumerate(((Kp, CUM_EPS), (KVp, 0.0))):
                dve.memset(buf[:, :, :, 0:1], v).then_inc(s_zero, 1)
            dve.memset(Ep[:, :, :, 0:2], 0.0).then_inc(s_zero, 1)
            dve.memset(Mp[:, :, :, 1:2], 0.0).then_inc(s_zero, 1)
            dve.wait_ge(s_zero, 1)
            dve.memset(seq_mask[:, :].rearrange("p (s l) -> p s l", s=CS)[:, :, 0:1], 0.0).then_inc(s_zero, 1)
            dve.memset(lnbias[:, :], LN_SHIFT).then_inc(s_lnb, 1)

            def stats(at, s, src, bn_t, mv_t):
                k = at.par
                wait(dve, s["norm"], CN * (at.c - 1))
                for t in range(CN):
                    dve.bn_stats(bn_t[:, k, t, :], src[:, k, t, :]).then_inc(s["bn"], 1)
                wait(dve, s["bn"], CN * (at.c + 1))
                alone(dve)
                for t in range(CN):
                    dve.bn_aggr(mv_t[:, k, t, :], bn_t[:, k, t, :]).then_inc(s["aggr"], 1)

            def first_stats(a):
                wait(dve, s_x[a.par], 16 * (a.half + 1))
                stats(a, sA, x_in, bn[0], mv[0])

            def group_of(g):
                wait(dve, s_gates, 2 * (g + 1))
                lg = ps_gate[:, 0:GT * E].rearrange("p (t e) -> p t e", e=E)
                dve.tensor_reduce(top[:, :], lg, AX.X, ALU.max).then_inc(s_oh, 1)
                wait(dve, s_oh, 5 * g + 1)
                dve.tensor_tensor(is_top[:, :, :], lg, top[:, :].unsqueeze(2).to_broadcast([P, GT, E]),
                                  ALU.is_equal).then_inc(s_oh, 1)
                wait(dve, s_oh, 5 * g + 2)
                dve.tensor_tensor(is_top[:, :, :], is_top[:, :, :], expert_no[:, :, :], ALU.mult).then_inc(s_oh, 1)
                wait(dve, s_oh, 5 * g + 3)
                dve.tensor_reduce(pick[:, :], is_top[:, :, :], AX.X, ALU.min).then_inc(s_oh, 1)
                wait(dve, s_oh, 5 * g + 4)
                dve.tensor_scalar(pick_c[:, :], pick[:, :], -1.0, None, ALU.min).then_inc(s_oh, 1)
                wait(dve, s_oh, 5 * g + 5)
                dve.tensor_tensor(onehot[:, :, :], expert_no[:, :, :],
                                  pick_c[:, :].unsqueeze(2).to_broadcast([P, GT, E]),
                                  ALU.is_equal).then_inc(s_ohr, 1)

            def slots_of(g):
                n = GT * E
                wait(dve, s_rank, g + 1)
                dve.tensor_copy(run_in[:, :, 0:1], run_out[:, :, GT:GT + 1]).then_inc(s_run, 1)
                dve.tensor_copy(run_in[:, :, 1:GT + 1],
                                ps_gate[:, 2 * n:3 * n].rearrange("p (e t) -> p e t", e=E)).then_inc(s_run, 1)
                wait(dve, s_run, 5 * g + 2)
                dve.tensor_tensor_scan(run_out[:, :, :].rearrange("p e t -> p (e t)"), run_mask[:, :],
                                       run_in[:, :, :].rearrange("p e t -> p (e t)"), 0.0, ALU.mult,
                                       ALU.add).then_inc(s_run, 1)
                wait(dve, s_run, 5 * g + 3)
                dve.tensor_tensor(slot_f[:, :, :], ps_gate[:, n:2 * n].rearrange("p (e t) -> p e t", e=E),
                                  run_out[:, :, 0:GT], ALU.add).then_inc(s_run, 1)
                wait(dve, s_run, 5 * g + 4)
                dve.tensor_tensor(slot_m[:, :, :], slot_f[:, :, :], onehot[:, :, :].rearrange("p t e -> p e t"),
                                  ALU.mult).then_inc(s_run, 1)
                wait(dve, s_run, 5 * g + 5)
                for k in range(2):
                    wait(dve, s_scat[k], 16 * CN * g)
                dve.tensor_reduce(slots[:, :], slot_m[:, :, :].rearrange("p e t -> p t e"), AX.X,
                                  ALU.add).then_inc(s_slot, 1)

            def chunk(c):
                here = c.within(NC)
                k = c.par
                if here:
                    if c.fixed and c.c == 0:
                        dve.wait_ge(s_zero, 6)
                    wait(dve, s_K, c.c + 1)
                    dve.tensor_tensor_scan(Kc[:, k, :, :].rearrange("p s l -> p (s l)"), seq_mask[:, :],
                                           Kp[:, k, :, :].rearrange("p s l -> p (s l)"), 0.0,
                                           ALU.mult, ALU.add).then_inc(s_Kc, 1)
                    wait(dve, s_KV, c.c + 1)
                    dve.tensor_tensor_scan(Sc[:, k, :, :].rearrange("p s l -> p (s l)"), seq_mask[:, :],
                                           KVp[:, k, :, :].rearrange("p s l -> p (s l)"), 0.0,
                                           ALU.mult, ALU.add).then_inc(s_Sc, 1)
                s = c + (-4)
                if s.par == 0 and s.within(NC):
                    slots_of(s.half)
                a = c + 2
                if a.within(NC):
                    first_stats(a)
                o = c + (-1)
                if o.within(NC):
                    wait(dve, s_proj, o.c + 1)
                    wait(dve, s_xr[o.par], 16 * (o.half + 1))
                    wait(dve, s_x1out[o.par], 16 * o.half)
                    wait(dve, sB["norm"], CN * (o.c - 1))
                    dve.tensor_tensor(x1_sb[:, o.par, :, :], ps_proj[:, :].rearrange("p (t d) -> p t d", t=CN),
                                      x_res[:, o.par, :, :], ALU.add).then_inc(s_x1, 1)
                    wait(dve, s_x1, o.c + 1)
                    stats(o, sB, x1_sb, bn[1], mv[1])
                if here:
                    wait(dve, s_SR, c.c + 1)
                    dve.scalar_tensor_tensor(out=Oar[:, k, :, 1:LP], in0=tq[:, k, :, 1:LP], scalar=1.0,
                                             in1=SRp[:, k, :, 1:LP], op0=ALU.add, op1=ALU.mult).then_inc(s_Oar, 1)
                    wait(dve, s_Oar, c.c + 1)
                    dve.scalar_tensor_tensor(out=Ep[:, k, :, 2:LP], in0=Oar[:, k, :, 1:L], scalar=-0.5,
                                             in1=hT[:, k, :, 2:LP], op0=ALU.mult, op1=ALU.add).then_inc(s_E, 1)
                    wait(dve, s_E, c.c + 1)
                    dve.scalar_tensor_tensor(out=Ep[:, k, :, 2:LP], in0=t2[:, k, :, 1:L], scalar=1.0,
                                             in1=Ep[:, k, :, 2:LP], op0=ALU.add, op1=ALU.mult).then_inc(s_KE, 1)
                    wait(dve, s_KE, c.c + 1)
                    dve.tensor_tensor_scan(S2[:, k, :, :].rearrange("p s l -> p (s l)"), seq_mask[:, :],
                                           Ep[:, k, :, :].rearrange("p s l -> p (s l)"), 0.0,
                                           ALU.mult, ALU.add).then_inc(s_S2, 1)
                    wait(dve, s_S2, c.c + 1)
                    dve.scalar_tensor_tensor(out=Mp[:, k, :, 2:LP], in0=tq[:, k, :, 1:L], scalar=1.0,
                                             in1=S2[:, k, :, 2:LP], op0=ALU.add, op1=ALU.mult).then_inc(s_M, 1)
                    wait(dve, s_M, c.c + 1)
                    wait(dve, s_proj, c.c - 1)
                    dve.scalar_tensor_tensor(out=Ot[:, k, :, :], in0=Mp[:, k, :, 1:LP], scalar=0.5 * KAPPA,
                                             in1=Oar[:, k, :, 1:LP], op0=ALU.mult, op1=ALU.add).then_inc(s_O, 1)
                r = c + (-2)
                if r.par == 1 and r.within(NC):
                    if r.fixed and r.c == 1:
                        dve.wait_ge(s_iota, 9 + 2 * E + 1)
                    group_of(r.half)

            dve.wait_ge(s_small, 16 * 10)
            dve.wait_ge(s_th, 1)
            dve.scalar_tensor_tensor(out=cond_silu[:, :], in0=cond_th[:, :], scalar=1.0, in1=cond_sb[:, :],
                                     op0=ALU.add, op1=ALU.mult).then_inc(s_silu, 1)
            first_stats(At(0, 0, 0))
            first_stats(At(1, 0, 1))
            dve.wait_ge(s_setup_pe, 6)
            for n in range(4):
                dve.tensor_scalar(mod[:, n, :], ps_k2[:, n * B:(n + 1) * B], float(n % 2), None,
                                  ALU.add).then_inc(s_modw, 1)
            dve.wait_ge(s_modw, 4)
            dve.wait_ge(s_setup_pe, 7)
            g2 = ps_proj[0:B, 0:2 * D].rearrange("p (g d) -> p g d", g=2)
            dve.tensor_copy(gate_raw[:, :, :], g2).then_inc(s_gate, 1)
            dve.wait_ge(s_gate, 1)
            dve.tensor_scalar(gate_sign[:, :, :], gate_raw[:, :, :], 0.0, 2.0, ALU.is_ge, ALU.mult).then_inc(s_gate, 1)
            dve.scalar_tensor_tensor(out=gate_abs[:, :, :], in0=gate_raw[:, :, :], scalar=-1.0,
                                     in1=gate_raw[:, :, :], op0=ALU.mult, op1=ALU.max).then_inc(s_gate, 1)
            dve.wait_ge(s_gate, 3)
            dve.tensor_scalar(gate_abs[:, :, :], gate_abs[:, :, :], 0.25, None, ALU.max).then_inc(s_gabs, 1)
            dve.wait_ge(s_gabs, 1)
            dve.scalar_tensor_tensor(out=gates[:, 0:2, :], in0=gate_sign[:, :, :], scalar=-1.0,
                                     in1=gate_abs[:, :, :], op0=ALU.add, op1=ALU.mult).then_inc(s_gate, 1)
            dve.wait_ge(s_gate, 4)
            dve.tensor_tensor(gates[:, 2, :], gates[:, 0, :], bproj_bc[:, :], ALU.mult).then_inc(s_gate, 1)
            dve.wait_ge(s_gate, 5)
            dve.tensor_scalar(gates[:, 0, :], gates[:, 0, :], 0.5, None, ALU.mult).then_inc(s_gate, 1)
            dve.wait_ge(s_gin, 32)
            dve.wait_ge(s_setup_act, 1)
            dve.tensor_tensor(wg[:, :, :], wg[:, :, :], wT[:, 3:4, :].to_broadcast([P, B, D]),
                              ALU.mult).then_inc(s_wg, 1)
            walk(dve, *(0,) + A_SPAN[1:], chunk)

            dve.wait_ge(s_slot, NT // GT)
            step = [0]

            def then(ins):
                step[0] += 1
                ins.then_inc(s_plan, 1)
                dve.wait_ge(s_plan, step[0])

            dve.tensor_copy(end_i[:, :], run_out[:, :, GT]).then_inc(s_count, 1)
            then(dve.tensor_tensor(count_f[:, :], run_out[:, :, GT], region[:, 0:E], ALU.subtract))
            then(dve.tensor_scalar(count_i[:, :], count_f[:, :], float(FT - 1), None, ALU.add))
            then(dve.tensor_scalar(tiles_i[:, :], count_i[:, :], FT.bit_length() - 1, None, ALU.arith_shift_right))
            then(dve.tensor_copy(tiles_f[:, :], tiles_i[:, :]))
            then(dve.tensor_tensor_scan(tiles_end[:, :], run_mask[:, 1:E + 1], tiles_f[:, :], 0.0, ALU.mult, ALU.add))
            then(dve.scalar_tensor_tensor(out=shift[:, 1:E + 1], in0=tiles_end[:, :], scalar=-float(FT),
                                          in1=region[:, 1:E + 1], op0=ALU.mult, op1=ALU.add))
            then(dve.memset(shift[:, 0:1], 0.0))
            then(dve.tensor_tensor(past[:, :, :], tile_no[:, :].unsqueeze(2).to_broadcast([P, NJ, E]),
                                   tiles_end[:, :].unsqueeze(1).to_broadcast([P, NJ, E]), ALU.is_ge))
            then(dve.tensor_reduce(tile_e[:, :], past[:, :, :], AX.X, ALU.add))
            then(dve.tensor_scalar(tile_ec[:, :], tile_e[:, :], float(E - 1), None, ALU.min))
            dve.tensor_scalar(sel[:, :], tile_ec[0:E, :], part_no[0:E, :], None, ALU.is_equal).then_inc(s_planned, 1)
            for e in range(E + 1):
                dve.tensor_scalar(is_e[:, :, e], tile_e[:, :], float(e), None, ALU.is_equal).then_inc(s_ise, 1)
            dve.wait_ge(s_ise, E + 1)
            then(dve.tensor_tensor(is_e[:, :, :], is_e[:, :, :],
                                   shift[:, :].unsqueeze(1).to_broadcast([P, NJ, E + 1]), ALU.mult))
            then(dve.tensor_reduce(row_f[:, :], is_e[:, :, :], AX.X, ALU.add))
            then(dve.scalar_tensor_tensor(out=row_g[:, :], in0=tile_no[:, :], scalar=float(FT), in1=row_f[:, :],
                                          op0=ALU.mult, op1=ALU.add))
            then(dve.tensor_copy(plan[:, :, 0], tile_ec[:, :]))
            dve.tensor_scalar(plan[:, :, 1], row_g[:, :], float(E * RS), None, ALU.min).then_inc(s_planned, 1)
            dve.wait_ge(s_par, 1)

            def expert_tile(j):
                if j.within(NJ):
                    k = j.par
                    wait(dve, b_l1[1], j.c + 1)
                    wait(dve, b_y, j.c - 1)
                    for f in range(2):
                        a = dve.tensor_scalar(hid[:, k, 2 + f, :], ps_h[:, f * FT:(f + 1) * FT],
                                              par[:, 5 + f, bass.ds(j.c, 1)], 0.0, ALU.add, ALU.max)
                    a.then_inc(b_hidD, 1)
                u = j + (-1)
                if u.within(NJ):
                    k = u.par
                    wait(dve, b_up, u.c + 1)
                    wait(dve, s_uout[k], 16 * FS * u.half)
                    dve.tensor_tensor(u_sb[:, k, :, :], ps_k2[:, 0:FT].rearrange("p (s d) -> p s d", s=FS),
                                      rows_all[:, bass.ds(u.c, 1), :, 0:D].rearrange("p j s d -> p (j s) d"),
                                      ALU.add).then_inc(b_u, 1)
                z = j + 2
                if z.within(NJ):
                    k = z.par
                    wait(dve, b_rstd, z.c + 1)
                    wait(dve, b_zTp, z.c - 1)
                    for t in range(FS):
                        dve.tensor_scalar(bz[:, k, t, :], rows_all[:, bass.ds(z.c, 1), t, 0:D]
                                          .rearrange("p j d -> p (j d)"), bmv[:, k, t, 0:1], brstd[:, k, t:t + 1],
                                          ALU.subtract, ALU.mult).then_inc(b_z, 1)
                n = j + 3
                if n.within(NJ):
                    k = n.par
                    wait(dve, s_rin[k], 16 * (n.half + 1))
                    alone(dve)
                    for t in range(FS):
                        dve.bn_stats(bbn[:, k, t, :], rows_all[:, bass.ds(n.c, 1), t, 0:D]
                                     .rearrange("p j d -> p (j d)")).then_inc(b_bn, 1)
                    wait(dve, b_bn, FS * (n.c + 1))
                    wait(dve, b_z, FS * (n.c - 1))
                    alone(dve)
                    for t in range(FS):
                        dve.bn_aggr(bmv[:, k, t, :], bbn[:, k, t, :]).then_inc(b_aggr, 1)

            walk(dve, *B_SPAN, expert_tile)

            dve.wait_ge(s_gbin, 16)
            for g in range(NT // GT):
                dve.wait_ge(s_uin[g % 4], 32 * (g // 4 + 1))
                v = uc[:, g % 4, :, :].rearrange("p (b t) d -> p b t d", t=L // P)
                nb = GT * P // L
                for b in range(nb):
                    dve.tensor_tensor(v[:, b, :, :], v[:, b, :, :],
                                      gb_bc[:, g * nb + b:g * nb + b + 1, :].to_broadcast([P, L // P, D]),
                                      ALU.mult).then_inc(c_mul, 1)
                dve.wait_ge(c_mul, nb * (g + 1))
                xc = x1c[:, g % 4, :, :]
                dve.tensor_tensor(xc, xc, uc[:, g % 4, :, :], ALU.add).then_inc(c_add, 1)


_INS = ['L0_attn_x', 'L0_attn_Wq1', 'L0_attn_bq1', 'L0_attn_Wk1', 'L0_attn_bk1', 'L0_attn_Wk2', 'L0_attn_bk2',
        'L0_attn_Wproj', 'L0_attn_bproj', 'L0_ffn_centroids', 'L0_ffn_ln_g', 'L0_ffn_ln_b', 'L0_ffn_W1',
        'L0_ffn_b1', 'L0_ffn_W2', 'L0_ffn_b2', 'L0_c', 'L0_wmod']
_OUTS = [((32, 256, 128), 'float32')]


def kernel(**inputs):
    import numpy as _np
    import concourse.bacc as _bacc
    from concourse import mybir as _mybir
    from concourse.bass_utils import run_bass_kernel_spmd as _run

    nc = _bacc.Bacc("TRN2", target_bir_lowering=False, num_devices=1)
    arrays, args = {}, []
    for name in _INS:
        a = _np.ascontiguousarray(inputs[name])
        arrays[f"in_{name}_dram"] = a
        args.append(nc.dram_tensor(f"in_{name}_dram", a.shape, _mybir.dt.from_np(a.dtype), kind="ExternalInput").ap())
    for i, (shape, dtype) in enumerate(_OUTS):
        dt = _mybir.dt.from_np(_np.dtype(dtype))
        args.append(nc.dram_tensor(f"out_{i}_dram", shape, dt, kind="ExternalOutput").ap())
    build_block(nc, *args)
    r = _run(nc, [arrays], core_ids=[0])
    got = tuple(r.results[0][f"out_{i}_dram"] for i in range(len(_OUTS)))
    return got[0]
```

```python
from contextlib import ExitStack

import numpy as np

import concourse.bass as bass
from concourse import mybir


P = 128
F32 = mybir.dt.float32
BF16 = mybir.dt.bfloat16
I32 = mybir.dt.int32
ALU = mybir.AluOpType
ACT = mybir.ActivationFunctionType
AX = mybir.AxisListType
LN_EPS = 1e-5
CUM_EPS = 1e-6
MA_SLOPE = 0.02
MA_K = 0.02
LN_SCALE = 2.0 ** -44
LN_SHIFT = -44 * 0.6931471805599453


def build_block(nc, x, Wq1, bq1, Wk1, bk1, Wk2, bk2, Wproj, bproj, centroids, ln_g, ln_b,
                W1, b1, W2, b2, cond, wmod, out):
    B, L, D = x.shape
    E, _, F = W1.shape
    T = B * L
    NT = T // P
    CS = 2
    CT = CS * L
    CN = CT // P
    NC = T // CT
    GT = 2 * CN
    LP = L + 1
    FT = 2 * P
    FS = FT // P
    NJ = T // FT + E - 1
    FC = F // P
    RS = T + FT
    W = D + 1
    AHEAD = 3
    NV = 3 + FC
    ISQ = float(D) ** -0.5
    KAPPA = MA_SLOPE * ISQ
    assert D == P and NC % 2 == 0 and B == 32

    xt = x.rearrange("b l d -> (b l) d").rearrange("(t p) d -> p t d", p=P)
    ot = out.rearrange("b l d -> (b l) d").rearrange("(t p) d -> p t d", p=P)
    W1f = W1.rearrange("e d f -> (e d) f")
    W2f = W2.rearrange("e f d -> (e f) d")
    rows_dram = nc.dram_tensor("expert_rows", ((E + 1) * RS, W), F32, kind="Internal").ap()
    x1_dram = nc.dram_tensor("x1", (T, D), F32, kind="Internal").ap()
    u_dram = nc.dram_tensor("expert_out", (T, D), F32, kind="Internal").ap()
    gates_dram = nc.dram_tensor("gates_rows", (3, B, D), F32, kind="Internal").ap()

    with ExitStack() as ctx:
        def sb(name, shape, dt=F32):
            return ctx.enter_context(nc.sbuf_tensor(name, shape, dt))

        def sem(name):
            return ctx.enter_context(nc.semaphore(name))

        ctx.enter_context(nc.allow_non_contiguous_dma(reason="biases are loaded as columns"))
        ctx.enter_context(nc.allow_low_precision(reason="numbers of slots are whole and below 2^24"))

        bank = [ctx.enter_context(nc.psum_tensor(f"bank{i}", [P, 512], F32)) for i in range(8)]
        ps_x, ps_q, ps_k, ps_k2, ps_proj, ps_z, ps_h, ps_gate = bank

        ident = sb("ident", [P, P])
        lower = sb("lower", [P, P], BF16)
        ones_bf = sb("ones_bf", [P, P], BF16)
        ones_row = sb("ones_row", [1, P])
        expert_no = sb("expert_no", [P, GT, E])
        tile_no = sb("tile_no", [P, NJ])
        part_no = sb("part_no", [P, 1])
        part_i = sb("part_i", [P, 1], I32)
        iota_i = sb("iota_i", [P, GT, E], I32)
        iota_j = sb("iota_j", [P, NJ], I32)
        token_no = sb("token_no", [P, NT], I32)
        pad_rows = sb("pad_rows", [P, FS, W])
        neg_half = sb("neg_half", [P, CN])
        seq_mask = sb("seq_mask", [P, CS * LP])
        run_mask = sb("run_mask", [P, E * (GT + 1)])
        w_raw = sb("w_raw", [P, 4, P])
        wT = sb("wT", [P, 4, P])
        bias_raw = sb("bias_raw", [P, 3])
        bias = sb("bias", [P, 3])
        cent_raw = sb("cent_raw", [E, D])
        centT = sb("centT", [P, E])
        cond_sb = sb("cond_sb", [B, D])
        cond_th = sb("cond_th", [B, D])
        cond_silu = sb("cond_silu", [B, D])
        condT = sb("condT", [P, B])
        wmod_sb = sb("wmod_sb", [P, 6 * D])
        mod = sb("mod", [P, 4, B])
        gate_raw = sb("gate_raw", [B, 2, D])
        gate_sign = sb("gate_sign", [B, 2, D])
        gate_abs = sb("gate_abs", [B, 2, D])
        gates = sb("gates", [B, 3, D])
        bproj_bc = sb("bproj_bc", [B, D])
        shared = sb("shared", [P, max(2 * B * D, NJ * FS * W)])
        wg = shared[:, 0:B * D].rearrange("p (b d) -> p b d", b=B)
        gbp_row = shared[0:1, B * D:2 * B * D].rearrange("p (b d) -> p b d", b=B)
        rows_all = shared[:, 0:NJ * FS * W].rearrange("p (j s w) -> p j s w", j=NJ, s=FS)
        gb_bc = sb("gb_bc", [P, B, D])
        lnbias = sb("lnbias", [P, 1])
        epsv = sb("epsv", [P, 1])
        params = sb("params", [E, NV * D])

        x_in = sb("x_in", [P, 2, CN, D])
        x_res = sb("x_res", [P, 2, CN, D])
        x1_sb = sb("x1_sb", [P, 2, CN, D])
        work = sb("work", [P, 13 * 2 * CS * LP])
        used = [0]

        def carve(shape):
            a, n = used[0], int(np.prod(shape))
            used[0] += n
            names = " ".join("abcd"[:len(shape)])
            return work[:, a:a + n].rearrange(f"p ({names}) -> p {names}", **dict(zip("abcd", shape)))

        xh = sb("xh", [P, 2, CN, D])
        hT = carve([2, CS, LP])
        Kp = carve([2, CS, LP])
        KVp = carve([2, CS, LP])
        tq = carve([2, CS, LP])
        t2 = carve([2, CS, LP])
        Kc = carve([2, CS, LP])
        lnK = carve([2, CS, LP])
        SRp = carve([2, CS, LP])
        Sc = carve([2, CS, LP])
        Oar = carve([2, CS, LP])
        Ep = carve([2, CS, LP])
        S2 = carve([2, CS, LP])
        Mp = carve([2, CS, LP])
        Ot = sb("Ot", [P, 2, CS, L])
        zz = sb("zz", [P, 2, CN, D])
        h2T = sb("h2T", [P, 2, CT])
        rows = sb("rows", [P, 2, CN, W])
        bn = [sb(f"bn{i}", [P, 2, CN, 6]) for i in range(2)]
        mv = sb("mv", [P, 2, 2, CN, 2])
        lnv = sb("lnv", [P, 2, 2, CN])
        rstd = sb("rstd", [P, 2, 2, CN])
        negm = sb("negm", [P, 2, CN])
        top = sb("top", [P, GT])
        is_top = sb("is_top", [P, GT, E])
        pick = sb("pick", [P, GT])
        pick_c = sb("pick_c", [P, GT])
        onehot = sb("onehot", [P, GT, E], BF16)
        run_in = sb("run_in", [P, E, GT + 1])
        run_out = sb("run_out", [P, E, GT + 1])
        slot_f = sb("slot_f", [P, E, GT])
        slot_m = sb("slot_m", [P, E, GT])
        slots = sb("slots", [P, GT], I32)
        count_f = sb("count_f", [P, E])
        region = sb("region", [P, E + 1])
        count_i = sb("count_i", [P, E], I32)
        end_i = sb("end_i", [P, E], I32)
        tiles_i = sb("tiles_i", [P, E], I32)
        tiles_f = sb("tiles_f", [P, E])
        tiles_end = sb("tiles_end", [P, E])
        shift = sb("shift", [P, E + 1])
        past = sb("past", [P, NJ, E])
        tile_e = sb("tile_e", [P, NJ])
        tile_ec = sb("tile_ec", [P, NJ])
        is_e = sb("is_e", [P, NJ, E + 1])
        row_f = sb("row_f", [P, NJ])
        row_g = sb("row_g", [P, NJ])
        plan = sb("plan", [P, NJ + AHEAD, 2], I32)
        sel = sb("sel", [E, NJ])
        par = sb("par", [P, NV, NJ])
        used[0] = 0
        mail = sb("mail", [1, 2, 2], I32)
        w1_sb = carve([2, F])
        w2_sb = carve([2, FC, D])
        bbn = sb("bbn", [P, 2, FS, 6])
        bmv = sb("bmv", [P, 2, FS, 2])
        bveps = sb("bveps", [P, 2, FS])
        brstd = sb("brstd", [P, 2, FS])
        bz = carve([2, FS, D])
        zT = carve([2, FT])
        hid = carve([2, FC, FT])
        yT = carve([2, FT])
        u_sb = carve([2, FS, D])
        ids = sb("ids", [P, 2, FS], I32)
        uc = carve([4, GT, D])
        x1c = sb("x1c", [P, 4, GT, D])

        s_w = sem("weights_in"); s_small = sem("small_in"); s_cond = sem("cond_in"); s_mod_in = sem("mod_in")
        s_x = [sem(f"x_in{i}") for i in range(2)]
        s_xr = [sem(f"x_res{i}") for i in range(2)]
        s_x1out = [sem(f"x1_out{i}") for i in range(2)]
        s_const = sem("constants"); s_ident = sem("ident_ready"); s_iota = sem("iota_ready")
        s_pads = sem("pads_ready"); s_zero = sem("leading_columns")
        s_setup_pe = sem("setup_pe"); s_setup_act = sem("setup_act"); s_modw = sem("mod_ready"); s_lnb = sem("ln_shift_ready")
        s_th = sem("cond_tanh"); s_silu = sem("cond_silu"); s_gate = sem("gate_steps"); s_gabs = sem("gate_abs"); s_ise = sem("is_expert"); s_tok = sem("token_numbers")
        s_gout = sem("gates_out"); s_gin = sem("gates_in"); s_gbin = sem("gb_in"); s_wg = sem("wg_ready")
        sA = {n: sem("x_" + n) for n in ("bn", "aggr", "norm")}
        sB = {n: sem("z_" + n) for n in ("bn", "aggr", "norm")}
        s_lnv = sem("ln_var_ready"); s_rstd = sem("rstd_ready"); s_negm = sem("neg_mean_ready")
        s_xT = sem("xT_psum"); s_hT = sem("hT_ready"); s_qkv = sem("qkv_psum")
        s_tq = sem("tq_ready"); s_t2 = sem("t2_ready"); s_K = sem("K_ready"); s_KV = sem("KV_ready")
        s_Kc = sem("Kc_ready"); s_Sc = sem("Sc_ready"); s_ln = sem("lnK_ready"); s_R = sem("R_ready")
        s_SR = sem("SR_ready"); s_Oar = sem("Oar_ready"); s_E = sem("E_ready"); s_KE = sem("KE_ready")
        s_S2 = sem("S2_ready"); s_M = sem("M_ready"); s_O = sem("O_ready")
        s_proj = sem("proj_psum"); s_x1 = sem("x1_ready")
        s_zT = sem("zT_psum"); s_h2T = sem("h2T_ready"); s_h2 = sem("h2_psum"); s_row = sem("rows_ready")
        s_gates = sem("logits_psum"); s_oh = sem("onehot_steps"); s_ohr = sem("onehot_ready")
        s_rank = sem("rank_psum"); s_run = sem("run_steps"); s_slot = sem("slots_ready")
        s_scat = [sem(f"rows_scattered{i}") for i in range(2)]
        s_plan = sem("plan_steps"); s_planned = sem("plan_ready"); s_sel = sem("params_psum")
        s_par = sem("params_ready"); s_count = sem("counts_ready"); s_pad_out = sem("pads_out")
        s_mail = sem("mail_ready"); s_read = sem("mail_read")
        s_rin = [sem(f"rows_in{i}") for i in range(2)]
        s_win = [sem(f"expert_in{i}") for i in range(2)]
        b_bn = sem("b_bn"); b_aggr = sem("b_aggr"); b_veps = sem("b_veps"); b_rstd = sem("b_rstd")
        b_z = sem("b_z"); b_zTp = sem("b_zT_psum"); b_zT = sem("b_zT_ready")
        b_l1 = [sem(f"b_hidden_psum{i}") for i in range(2)]
        b_hidA = sem("b_hidden_act"); b_hidD = sem("b_hidden_dve")
        b_y = sem("b_y_psum"); b_yT = sem("b_yT_ready"); b_up = sem("b_u_psum"); b_u = sem("b_u_ready")
        b_ids = sem("b_ids_ready")
        s_uout = [sem(f"u_out{i}") for i in range(2)]
        s_uin = [sem(f"u_in{i}") for i in range(4)]
        c_mul = sem("c_mul"); c_add = sem("c_add")
        s_out = [sem(f"out_done{i}") for i in range(4)]

        def alone(eng):
            eng.sem_inc(s_met[eng], 1)

        def wait(eng, s, value):
            if isinstance(value, int) and value <= 0:
                return
            eng.wait_ge(s, value)

        class At:

            def __init__(self, c, half, par):
                self.c, self.half, self.par = c, half, par
                self.fixed = isinstance(c, int)

            def __add__(self, o):
                k = self.par + o
                return At(self.c + o, self.half + k // 2, k % 2)

            def within(self, n):
                return not self.fixed or 0 <= self.c < n

        def walk(eng, first, lo, hi, last, body):
            for c in range(first, lo):
                body(At(c, c // 2, c % 2))
            with eng.Fori(lo // 2, hi // 2) as i:
                at = At(i * 2 + lo % 2, i, lo % 2)
                body(at)
                body(at + 1)
            for c in range(hi, last):
                body(At(c, c // 2, c % 2))

        A_SPAN = (-4, 7, 11, NC + 5)
        B_SPAN = (-5, 4, 36, NJ + 1)

        s_met = {eng: sem(f"met_{n}") for n, eng in (("pool", nc.gpsimd), ("dve", nc.vector), ("sp", nc.sync))}
        block = ctx.enter_context(nc.Block())

        @block.sync
        def _(sp):
            for k in range(2):
                sp.dma_start(x_in[:, k, :, :], xt[:, k * CN:(k + 1) * CN, :]).then_inc(s_x[k], 16)
            for n, w in enumerate((Wq1, Wk1, Wk2, Wproj)):
                sp.dma_start(w_raw[:, n, :], w).then_inc(s_w, 16)
            sp.wait_ge(s_gate, 6)
            sp.dma_start(gates_dram.rearrange("g b d -> b g d"), gates[:, :, :]).then_inc(s_gout, 16)
            sp.wait_ge(s_gout, 16)
            sp.dma_start(wg[:, :, :].rearrange("p b d -> p (b d)"),
                         gates_dram[0].rearrange("b d -> (b d)").partition_broadcast(P)).then_inc(s_gin, 16)
            sp.dma_start(gbp_row[:, :, :].rearrange("o b d -> o (b d)"),
                         gates_dram[2].rearrange("b d -> (b d)").partition_broadcast(1)).then_inc(s_gin, 16)

            x1t = x1_dram.rearrange("(t p) d -> p t d", p=P)

            def stream(c):
                m = c + 5
                if m.within(NC):
                    wait(sp, sA["norm"], CN * (m.c - 1))
                    alone(sp)
                    wait(sp, s_x[m.par], 16 * m.half)
                    alone(sp)
                    sp.dma_start(x_in[:, m.par, :, :], xt[:, bass.ds(m.c * CN, CN), :]).then_inc(s_x[m.par], 16)
                n = c + 1
                if n.within(NC):
                    wait(sp, s_x1, n.c - 1)
                    alone(sp)
                    wait(sp, s_xr[n.par], 16 * n.half)
                    alone(sp)
                    sp.dma_start(x_res[:, n.par, :, :], xt[:, bass.ds(n.c * CN, CN), :]).then_inc(s_xr[n.par], 16)
                o = c + (-1)
                if o.within(NC):
                    wait(sp, s_x1, o.c + 1)
                    alone(sp)
                    wait(sp, s_x1out[o.par], 16 * o.half)
                    alone(sp)
                    sp.dma_start(x1t[:, bass.ds(o.c * CN, CN), :], x1_sb[:, o.par, :, :]
                                 ).then_inc(s_x1out[o.par], 16)

            walk(sp, -3, 3, 11, NC + 1, stream)
            sp.dma_start(gb_bc[:, :, :].rearrange("p b d -> p (b d)"),
                         gates_dram[1].rearrange("b d -> (b d)").partition_broadcast(P)).then_inc(s_gbin, 16)

            sp.wait_ge(s_pads, 2)
            sp.dma_start(rows_dram[E * RS:E * RS + FT, :].rearrange("(s p) w -> p s w", p=P),
                         pad_rows[:, :, :]).then_inc(s_pad_out, 16)
            sp.wait_ge(s_count, 1)
            for e in range(E):
                end = sp.value_load(end_i[0:1, e:e + 1], min_val=e * RS, max_val=e * RS + T)
                sp.dma_start(rows_dram[bass.ds(end, FT), :].rearrange("(s p) w -> p s w", p=P),
                             pad_rows[:, :, :]).then_inc(s_pad_out, 16)
            sp.wait_ge(s_pad_out, 16 * (E + 1))
            for k in range(2):
                sp.wait_ge(s_scat[k], 16 * NT // 2)

            def load_tile(m):
                sp.wait_ge(s_mail, m.c + 1)
                alone(sp)
                e = sp.value_load(mail[0:1, m.par, 0:1], min_val=0, max_val=E - 1)
                r = sp.value_load(mail[0:1, m.par, 1:2], min_val=0, max_val=E * RS)
                sp.sem_inc(s_read, 1)
                if m.within(NJ):
                    wait(sp, s_rin[m.par], 16 * m.half)
                    alone(sp)
                    sp.dma_start(rows_all[:, bass.ds(m.c, 1), :, :].rearrange("p j s w -> p (j s) w"),
                                 rows_dram[bass.ds(r, FT), :].rearrange("(s p) w -> p s w", p=P)
                                 ).then_inc(s_rin[m.par], 16)
                j = m + (-AHEAD)
                if j.within(NJ):
                    wait(sp, b_y, j.c - 1)
                    alone(sp)
                    sp.dma_start(w1_sb[:, j.par, :], W1f[bass.ds(e * D, D), :]).then_inc(s_win[j.par], 16)
                    sp.dma_start(w2_sb[:, j.par, :, :],
                                 W2f[bass.ds(e * F, F), :].rearrange("(k p) d -> p k d", p=P)
                                 ).then_inc(s_win[j.par], 16)

            walk(sp, 0, 6, 38, NJ + AHEAD, load_tile)

            for k in range(2):
                sp.wait_ge(s_uout[k], 16 * FS * ((NJ + 1 - k) // 2))
                sp.wait_ge(s_x1out[k], 16 * NC // 2)
            ut = u_dram.rearrange("(t p) d -> p t d", p=P)
            for g in range(NT // GT):
                if g >= 4:
                    sp.wait_ge(s_out[g % 4], 16 * (g // 4))
                sp.dma_start(uc[:, g % 4, :, :], ut[:, g * GT:(g + 1) * GT, :]).then_inc(s_uin[g % 4], 16)
                sp.dma_start(x1c[:, g % 4, :, :], x1t[:, g * GT:(g + 1) * GT, :]).then_inc(s_uin[g % 4], 16)

        @block.gpsimd
        def _(pool):
            pool.memset(ident[:, :], 0.0).then_inc(s_ident, 1)
            pool.wait_ge(s_ident, 1)
            pool.affine_select(out=ident[:, :], in_=ident[:, :], compare_op=ALU.not_equal, fill=1.0,
                               base=0, pattern=[[-1, P]], channel_multiplier=1).then_inc(s_ident, 1)
            pool.memset(neg_half[:, :], -0.5).then_inc(s_const, 1)
            pool.memset(ones_row[:, :], 1.0).then_inc(s_const, 1)
            pool.memset(ones_bf[:, :], 1.0).then_inc(s_const, 1)
            pool.memset(lower[:, :], 1.0).then_inc(s_const, 1)
            pool.wait_ge(s_const, 4)
            pool.affine_select(out=lower[:, :], in_=lower[:, :], compare_op=ALU.is_gt, fill=0.0,
                               base=0, pattern=[[1, P]], channel_multiplier=-1).then_inc(s_const, 1)

            def number_rows(c, g, first):
                wait(pool, s_scat[first], 16 * CN * g)
                alone(pool)
                pool.tensor_copy(rows[:, first, :, D:W].bitcast(I32),
                                 token_no[:, bass.ds(c * CN, CN)].unsqueeze(2)).then_inc(s_tok, 1)
                wait(pool, s_tok, c + 1)
                wait(pool, s_row, c + 1)
                wait(pool, s_slot, g + 1)
                alone(pool)

            def chunk(c):
                s = c + (-5)
                if s.within(NC):
                    if s.fixed and s.c == 0:
                        pool.wait_ge(s_iota, 1)
                    number_rows(s.c, s.half, s.par)
                    for t in range(CN):
                        pool.indirect_dma_start(rows_dram, bass.IndirectOffsetOnAxis(
                            ap=slots[:, s.par * CN + t:s.par * CN + t + 1], axis=0),
                            rows[:, s.par, t, :], None).then_inc(s_scat[s.par], 16)
                q = c + 1
                if q.within(NC):
                    k = q.par
                    wait(pool, s_R, q.c + 1)
                    wait(pool, s_Sc, q.c + 1)
                    pool.tensor_tensor(SRp[:, k, :, 1:LP], Sc[:, k, :, 1:LP], lnK[:, k, :, 1:LP],
                                       ALU.mult).then_inc(s_SR, 1)
                a = c + 3
                if a.within(NC):
                    k = a.par
                    wait(pool, sA["aggr"], CN * (a.c + 1))
                    alone(pool)
                    pool.tensor_scalar(negm[:, k, :], mv[:, k, 0, :, 0], -1.0, 0.0, ALU.mult,
                                       ALU.add).then_inc(s_negm, 1)
                    wait(pool, s_xT, a.c - 1)
                    wait(pool, s_rstd, a.c + 1)
                    wait(pool, s_negm, a.c + 1)
                    alone(pool)
                    for t in range(CN):
                        pool.tensor_scalar(xh[:, k, t, :], x_in[:, k, t, :], negm[:, k, t:t + 1],
                                           rstd[:, k, 0, t:t + 1], ALU.add, ALU.mult).then_inc(sA["norm"], 1)
                n = c + 2
                if n.within(NC):
                    k = n.par
                    wait(pool, s_hT, 2 * (n.c + 1))
                    wait(pool, s_K, n.c + 1)
                    if n.fixed and n.c == 0:
                        pool.wait_ge(s_zero, 6)
                    pool.tensor_tensor(KVp[:, k, :, 1:LP], Kp[:, k, :, 1:LP], hT[:, k, :, 1:LP],
                                       ALU.mult).then_inc(s_KV, 1)

            pool.iota(token_no[:, :], pattern=[[P, NT]], base=0, channel_multiplier=1).then_inc(s_iota, 1)
            pool.iota(iota_i[:, :, :], pattern=[[0, GT], [1, E]], base=-E, channel_multiplier=0).then_inc(s_iota, 1)
            pool.iota(iota_j[:, :], pattern=[[1, NJ]], base=0, channel_multiplier=0).then_inc(s_iota, 1)
            pool.iota(part_i[:, :], pattern=[[0, 1]], base=0, channel_multiplier=1).then_inc(s_iota, 1)
            pool.memset(pad_rows[:, :, :], 0.0).then_inc(s_pads, 1)
            pool.wait_ge(s_pads, 1)
            pool.memset(pad_rows[:, :, D:W].bitcast(I32), T).then_inc(s_pads, 1)
            pool.memset(run_mask[:, :], 1.0).then_inc(s_iota, 1)
            pool.wait_ge(s_iota, 5)
            pool.tensor_copy(expert_no[:, :, :], iota_i[:, :, :]).then_inc(s_iota, 1)
            pool.tensor_copy(tile_no[:, :], iota_j[:, :]).then_inc(s_iota, 1)
            pool.tensor_copy(part_no[:, :], part_i[:, :]).then_inc(s_iota, 1)
            pool.memset(run_mask[:, :].rearrange("p (e t) -> p e t", e=E)[:, :, 0:1], 0.0).then_inc(s_iota, 1)
            for e in range(E):
                pool.memset(run_out[:, e, GT:GT + 1], float(e * RS)).then_inc(s_iota, 1)
            for e in range(E + 1):
                pool.memset(region[:, e:e + 1], float(e * RS)).then_inc(s_iota, 1)
            walk(pool, *A_SPAN, chunk)

            def expert_step(j):
                m = j + 5
                if m.within(NJ + AHEAD):
                    if m.fixed and m.c == 0:
                        pool.wait_ge(s_planned, 2)
                    wait(pool, s_read, m.c - 1)
                    alone(pool)
                    pool.tensor_copy(mail[0:1, m.par, :],
                                     plan[0:1, bass.ds(m.c, 1), :].rearrange("p o w -> p (o w)")
                                     ).then_inc(s_mail, 1)
                n = j + 2
                if n.within(NJ):
                    k = n.par
                    wait(pool, b_aggr, FS * (n.c + 1))
                    alone(pool)
                    pool.tensor_scalar(bveps[:, k, :], bmv[:, k, :, 1], LN_EPS, None, ALU.add).then_inc(b_veps, 1)
                    wait(pool, b_veps, n.c + 1)
                    wait(pool, b_z, FS * (n.c - 1))
                    pool.tensor_tensor(brstd[:, k, :], bveps[:, k, :], neg_half[:, 0:FS], ALU.pow).then_inc(b_rstd, 1)
                u = j + (-1)
                if u.within(NJ):
                    k = u.par
                    wait(pool, s_uout[k], 16 * FS * u.half)
                    alone(pool)
                    pool.tensor_copy(ids[:, k, :], rows_all[:, bass.ds(u.c, 1), :, D:W].bitcast(I32)
                                     .rearrange("p j s w -> p (j s w)")).then_inc(b_ids, 1)
                    wait(pool, b_ids, u.c + 1)
                    wait(pool, b_u, u.c + 1)
                    alone(pool)
                    for t in range(FS):
                        pool.indirect_dma_start(u_dram, bass.IndirectOffsetOnAxis(ap=ids[:, k, t:t + 1], axis=0),
                                                u_sb[:, k, t, :], None, bounds_check=T - 1,
                                                oob_is_err=False).then_inc(s_uout[k], 16)

            walk(pool, *B_SPAN, expert_step)

        @block.tensor
        def _(pe):
            pe.wait_ge(s_ident, 2)
            pe.wait_ge(s_w, 64)
            for n in range(4):
                pe.transpose(ps_q[:, n * P:(n + 1) * P], w_raw[:, n, :], ident[:, :]).then_inc(s_setup_pe, 1)
            pe.wait_ge(s_silu, 1)
            pe.wait_ge(s_small, 16 * 9)
            pe.transpose(ps_k[:, 0:B], cond_silu[:, :], ident[0:B, 0:B])
            pe.transpose(ps_k[:, B:B + E], cent_raw[:, :], ident[0:E, 0:E]).then_inc(s_setup_pe, 1)
            pe.wait_ge(s_setup_act, 2)
            pe.wait_ge(s_mod_in, 16)
            for n, part in enumerate((0, 1, 3, 4)):
                mm = pe.matmul(ps_k2[:, n * B:(n + 1) * B], wmod_sb[:, part * D:(part + 1) * D], condT[:, :],
                               start=True, stop=True)
            mm.then_inc(s_setup_pe, 1)
            for n, part in enumerate((2, 5)):
                mm = pe.matmul(ps_proj[0:B, n * D:(n + 1) * D], condT[:, :], wmod_sb[:, part * D:(part + 1) * D],
                               start=True, stop=True)
            mm.then_inc(s_setup_pe, 1)
            pe.wait_ge(s_setup_act, 3)
            pe.wait_ge(s_modw, 4)
            pe.wait_ge(s_gate, 1)

            def ranks(g):
                wait(pe, s_ohr, g + 1)
                oh = onehot[:, :, :].rearrange("p t e -> p e t")
                pe.matmul(ps_gate[:, GT * E:2 * GT * E].rearrange("p (e t) -> p e t", e=E), lower[:, :], oh,
                          start=True, stop=True)
                pe.matmul(ps_gate[:, 2 * GT * E:3 * GT * E].rearrange("p (e t) -> p e t", e=E), ones_bf[:, :], oh,
                          start=True, stop=True).then_inc(s_rank, 1)

            def chunk(c):
                g = c + (-5)
                if g.par == 0 and g.within(NC):
                    if g.fixed and g.c == 0:
                        pe.wait_ge(s_const, 5)
                    ranks(g.half)
                z = c + (-3)
                if z.within(NC):
                    k = z.par
                    wait(pe, sB["norm"], CN * (z.c + 1))
                    wait(pe, s_h2T, 2 * z.c)
                    for t in range(CN):
                        mm = pe.transpose(ps_z[:, t * P:(t + 1) * P], zz[:, k, t, :], ident[:, :])
                    mm.then_inc(s_zT, 1)
                n = c + 2
                if n.within(NC):
                    wait(pe, sA["norm"], CN * (n.c + 1))
                    wait(pe, s_hT, 2 * n.c)
                    for t in range(CN):
                        mm = pe.transpose(ps_x[:, t * P:(t + 1) * P], xh[:, n.par, t, :], ident[:, :])
                    mm.then_inc(s_xT, 1)
                o = c + (-1)
                if o.within(NC):
                    if o.fixed and o.c == 0:
                        pe.wait_ge(s_wg, 1)
                    wait(pe, s_O, o.c + 1)
                    wait(pe, s_x1, o.c)
                    for t in range(CN):
                        s = t * P // L
                        seq = o.c * CS + s
                        dst = ps_proj[:, t * P:(t + 1) * P]
                        pe.matmul(dst, Ot[:, o.par, s, (t * P) % L:(t * P) % L + P],
                                  wg[:, bass.ds(seq, 1), :].rearrange("p o d -> p (o d)"), start=True, stop=False)
                        mm = pe.matmul(dst, ones_row[:, :],
                                       gbp_row[:, bass.ds(seq, 1), :].rearrange("p o d -> p (o d)"),
                                       start=False, stop=True)
                    mm.then_inc(s_proj, 1)
                if n.within(NC):
                    wait(pe, s_hT, 2 * (n.c + 1))
                    for m, (dst, free) in enumerate(((ps_k, s_K), (ps_q, s_tq), (ps_k2, s_t2))):
                        wait(pe, free, n.c)
                        pe.matmul(dst[:, :], wT[:, (1, 0, 2)[m], :], hT[:, n.par, :, 1:LP],
                                  start=True, stop=True).then_inc(s_qkv, 1)
                if z.within(NC):
                    wait(pe, s_h2T, 2 * (z.c + 1))
                    wait(pe, s_row, z.c)
                    for t in range(CN):
                        mm = pe.transpose(ps_h[:, t * P:(t + 1) * P], h2T[:, k, t * P:(t + 1) * P], ident[:, :])
                    mm.then_inc(s_h2, 1)
                    if k == 0:
                        wait(pe, s_slot, z.half)
                    for t in range(CN):
                        at = (k * CN + t) * E
                        mm = pe.matmul(ps_gate[:, at:at + E], h2T[:, k, t * P:(t + 1) * P], centT[:, :],
                                       start=True, stop=True)
                    mm.then_inc(s_gates, 1)

            walk(pe, *A_SPAN, chunk)

            pe.wait_ge(s_planned, 1)
            pe.wait_ge(s_small, 16 * 9)
            for n in range(NV):
                mm = pe.matmul(ps_x[:, n * NJ:(n + 1) * NJ], params[:, n * D:(n + 1) * D], sel[:, :],
                               start=True, stop=True)
            mm.then_inc(s_sel, 1)

            for s in (s_x1, s_row, s_K, s_tq, s_t2):
                pe.wait_ge(s, NC)
            pe.wait_ge(s_h2T, 2 * NC)

            def expert_tile(j):
                if j.within(NJ):
                    k = j.par
                    wait(pe, b_zT, j.c + 1)
                    wait(pe, s_win[k], 32 * (j.half + 1))
                    if j.fixed and j.c == 0:
                        pe.wait_ge(s_par, 1)
                    for f in range(FC):
                        if f == 0:
                            wait(pe, b_hidA, j.c)
                        if f == 2:
                            wait(pe, b_hidD, j.c)
                        mm = pe.matmul((ps_proj, ps_h)[f // 2][:, (f % 2) * FT:(f % 2 + 1) * FT],
                                       w1_sb[:, k, f * P:(f + 1) * P], zT[:, k, :], start=True, stop=True)
                        if f % 2:
                            mm.then_inc(b_l1[f // 2], 1)
                n = j + 1
                if n.within(NJ):
                    wait(pe, b_z, FS * (n.c + 1))
                    wait(pe, b_zT, n.c)
                    for t in range(FS):
                        mm = pe.transpose(ps_z[:, t * P:(t + 1) * P], bz[:, n.par, t, :], ident[:, :])
                    mm.then_inc(b_zTp, 1)
                u = j + (-1)
                if u.within(NJ):
                    wait(pe, b_yT, u.c + 1)
                    wait(pe, b_u, u.c)
                    for t in range(FS):
                        mm = pe.transpose(ps_k2[:, t * P:(t + 1) * P], yT[:, u.par, t * P:(t + 1) * P], ident[:, :])
                    mm.then_inc(b_up, 1)
                if j.within(NJ):
                    k = j.par
                    for f in range(FC):
                        if f == 0:
                            wait(pe, b_hidA, j.c + 1)
                        if f == 2:
                            wait(pe, b_hidD, j.c + 1)
                        mm = pe.matmul((ps_q, ps_k)[k][:, 0:FT], w2_sb[:, k, f, :], hid[:, k, f, :],
                                       start=(f == 0), stop=(f == FC - 1))
                    mm.then_inc(b_y, 1)

            walk(pe, *B_SPAN, expert_tile)

        @block.scalar
        def _(act):
            act.dma_start(cond_sb[:, :], cond).then_inc(s_cond, 16)
            act.dma_start(wmod_sb[:, :], wmod).then_inc(s_mod_in, 16)
            act.dma_start(cent_raw[:, :], centroids).then_inc(s_small, 16)
            for n, v in enumerate((bq1, bk2, bk1)):
                act.dma_start(bias_raw[:, n:n + 1], v.rearrange("(p o) -> p o", o=1)).then_inc(s_small, 16)
            act.dma_start(bproj_bc[:, :], bproj.partition_broadcast(B)).then_inc(s_small, 16)
            act.dma_start(params[:, 0:D], ln_g).then_inc(s_small, 16)
            act.dma_start(params[:, D:2 * D], ln_b).then_inc(s_small, 16)
            act.dma_start(params[:, 2 * D:3 * D], b2).then_inc(s_small, 16)
            act.dma_start(params[:, 3 * D:NV * D], b1).then_inc(s_small, 16)
            act.wait_ge(s_cond, 16)
            act.activation(cond_th[:, :], cond_sb[:, :], ACT.Tanh, scale=0.5).then_inc(s_th, 1)
            act.wait_ge(s_setup_pe, 4)
            act.activation(wT[:, :, :], ps_q[:, :].rearrange("p (n d) -> p n d", n=4), ACT.Copy).then_inc(s_setup_act, 1)
            act.wait_ge(s_setup_pe, 5)
            act.activation(condT[:, :], ps_k[:, 0:B], ACT.Copy, scale=0.5).then_inc(s_setup_act, 1)
            act.activation(centT[:, :], ps_k[:, B:B + E], ACT.Copy).then_inc(s_setup_act, 1)
            act.wait_ge(s_small, 16 * 9)
            act.mul(bias[:, 0:1], bias_raw[:, 0:1], 0.5).then_inc(s_setup_act, 1)
            act.mul(bias[:, 1:2], bias_raw[:, 1:2], 0.5 * MA_K * ISQ).then_inc(s_setup_act, 1)
            act.copy(bias[:, 2:3], bias_raw[:, 2:3]).then_inc(s_setup_act, 1)
            act.wait_ge(s_setup_act, 6)

            def chunk(c):
                z = c + (-3)
                if z.within(NC):
                    k = z.par
                    wait(act, s_zT, z.c + 1)
                    wait(act, s_gates, z.c - 1)
                    for s in range(CS):
                        act.activation(h2T[:, k, s * L:(s + 1) * L], ps_z[:, s * L:(s + 1) * L], ACT.Identity,
                                       bias=mod[:, 2, bass.ds(z.c * CS + s, 1)],
                                       scale=mod[:, 3, bass.ds(z.c * CS + s, 1)]).then_inc(s_h2T, 1)
                n = c + 2
                if n.within(NC):
                    if n.fixed and n.c == 0:
                        act.wait_ge(s_modw, 4)
                    wait(act, s_xT, n.c + 1)
                    wait(act, s_E, n.c - 1)
                    for s in range(CS):
                        act.activation(hT[:, n.par, s, 1:LP], ps_x[:, s * L:(s + 1) * L], ACT.Identity,
                                       bias=mod[:, 0, bass.ds(n.c * CS + s, 1)],
                                       scale=mod[:, 1, bass.ds(n.c * CS + s, 1)]).then_inc(s_hT, 1)
                q = c + 1
                k = q.par
                a, y = c + 3, c + (-2)
                kinds = slice(0 if a.within(NC) else 1, 2 if y.within(NC) else 1)
                if q.within(NC):
                    wait(act, s_Kc, q.c + 1)
                    act.activation(lnK[:, k, :, :], Kc[:, k, :, :], ACT.Ln, scale=LN_SCALE).then_inc(s_ln, 1)
                if a.within(NC) or y.within(NC):
                    if c.fixed and c.c == -3:
                        act.wait_ge(s_lnb, 2)
                    if a.within(NC):
                        wait(act, sA["aggr"], CN * (a.c + 1))
                        wait(act, sA["norm"], CN * (a.c - 1))
                    if y.within(NC):
                        wait(act, sB["aggr"], CN * (y.c + 1))
                        wait(act, sB["norm"], CN * (y.c - 1))
                    act.activation(lnv[:, k, kinds, :], mv[:, k, kinds, :, 1], ACT.Ln, bias=epsv[:, :]
                                   ).then_inc(s_lnv, 1)
                if q.within(NC):
                    wait(act, s_ln, q.c + 1)
                    act.activation(lnK[:, k, :, :], lnK[:, k, :, :], ACT.Exp, scale=-1.0,
                                   bias=lnbias[:, :]).then_inc(s_R, 1)
                if a.within(NC) or y.within(NC):
                    wait(act, s_lnv, c.c + 4)
                    act.activation(rstd[:, k, kinds, :], lnv[:, k, kinds, :], ACT.Exp, scale=-0.5
                                   ).then_inc(s_rstd, 1)
                if n.within(NC):
                    for m, (src, dst, f, b, scale, done) in enumerate((
                            (ps_k, Kp, ACT.Exp, 2, 1.0, s_K), (ps_q, tq, ACT.Tanh, 0, 0.5, s_tq),
                            (ps_k2, t2, ACT.Tanh, 1, 0.5 * MA_K * ISQ, s_t2))):
                        wait(act, s_qkv, 3 * n.c + m + 1)
                        if m == 1:
                            wait(act, s_M, n.c - 1)
                        if n.fixed and n.c == 0 and m == 0:
                            act.wait_ge(s_zero, 6)
                        act.activation(dst[:, n.par, :, 1:LP], src[:, :].rearrange("p (s l) -> p s l", s=CS), f,
                                       bias=bias[:, b:b + 1], scale=scale).then_inc(done, 1)
                if z.within(NC):
                    k = z.par
                    wait(act, s_h2, z.c + 1)
                    wait(act, s_scat[k], 16 * CN * z.half)
                    act.activation(rows[:, k, :, 0:D], ps_h[:, :].rearrange("p (t d) -> p t d", t=CN),
                                   ACT.Copy).then_inc(s_row, 1)

            walk(act, *A_SPAN, chunk)

            act.wait_ge(s_sel, 1)
            act.activation(par[:, :, :], ps_x[:, 0:NV * NJ].rearrange("p (v j) -> p v j", v=NV),
                           ACT.Copy).then_inc(s_par, 1)
            act.wait_ge(s_par, 1)

            def column(v, j):
                return par[:, v, bass.ds(j, 1)]

            def expert_tile(j):
                if j.within(NJ):
                    k = j.par
                    wait(act, b_l1[0], j.c + 1)
                    wait(act, b_y, j.c - 1)
                    for f in range(2):
                        a = act.activation(hid[:, k, f, :], ps_proj[:, f * FT:(f + 1) * FT], ACT.Relu,
                                           bias=column(3 + f, j.c))
                    a.then_inc(b_hidA, 1)
                n = j + 1
                if n.within(NJ):
                    wait(act, b_zTp, n.c + 1)
                    wait(act, b_l1[1], n.c - 1)
                    act.activation(zT[:, n.par, :], ps_z[:, 0:FT], ACT.Identity, bias=column(1, n.c),
                                   scale=column(0, n.c)).then_inc(b_zT, 1)
                if j.within(NJ):
                    wait(act, b_y, j.c + 1)
                    wait(act, b_up, j.c - 1)
                    act.activation(yT[:, k, :], (ps_q, ps_k)[k][:, 0:FT], ACT.Identity,
                                   bias=column(2, j.c)).then_inc(b_yT, 1)

            walk(act, *B_SPAN, expert_tile)

            for g in range(NT // GT):
                act.wait_ge(c_add, g + 1)
                act.dma_start(ot[:, g * GT:(g + 1) * GT, :], x1c[:, g % 4, :, :]).then_inc(s_out[g % 4], 16)
            for k in range(4):
                act.wait_ge(s_out[k], 16 * NT // GT // 4)

        @block.vector
        def _(dve):
            dve.memset(seq_mask[:, :], 1.0).then_inc(s_zero, 1)
            for k, (buf, v) in enumerate(((Kp, CUM_EPS), (KVp, 0.0))):
                dve.memset(buf[:, :, :, 0:1], v).then_inc(s_zero, 1)
            dve.memset(Ep[:, :, :, 0:2], 0.0).then_inc(s_zero, 1)
            dve.memset(Mp[:, :, :, 1:2], 0.0).then_inc(s_zero, 1)
            dve.wait_ge(s_zero, 1)
            dve.memset(seq_mask[:, :].rearrange("p (s l) -> p s l", s=CS)[:, :, 0:1], 0.0).then_inc(s_zero, 1)
            dve.memset(lnbias[:, :], LN_SHIFT).then_inc(s_lnb, 1)
            dve.memset(epsv[:, :], LN_EPS).then_inc(s_lnb, 1)

            def stats(at, s, src, kind):
                k = at.par if kind == 0 else 1 - at.par
                for t in range(CN):
                    dve.bn_stats(bn[kind][:, k, t, :], src[:, at.par, t, :]).then_inc(s["bn"], 1)

            def means(at, s, kind):
                k = at.par if kind == 0 else 1 - at.par
                wait(dve, s["norm"], CN * (at.c - 1))
                wait(dve, s["bn"], CN * (at.c + 1))
                alone(dve)
                for t in range(CN):
                    dve.bn_aggr(mv[:, k, kind, t, :], bn[kind][:, k, t, :]).then_inc(s["aggr"], 1)

            def group_of(g):
                wait(dve, s_gates, 2 * (g + 1))
                lg = ps_gate[:, 0:GT * E].rearrange("p (t e) -> p t e", e=E)
                dve.tensor_reduce(top[:, :], lg, AX.X, ALU.max).then_inc(s_oh, 1)
                wait(dve, s_oh, 5 * g + 1)
                dve.tensor_tensor(is_top[:, :, :], lg, top[:, :].unsqueeze(2).to_broadcast([P, GT, E]),
                                  ALU.is_equal).then_inc(s_oh, 1)
                wait(dve, s_oh, 5 * g + 2)
                dve.tensor_tensor(is_top[:, :, :], is_top[:, :, :], expert_no[:, :, :], ALU.mult).then_inc(s_oh, 1)
                wait(dve, s_oh, 5 * g + 3)
                dve.tensor_reduce(pick[:, :], is_top[:, :, :], AX.X, ALU.min).then_inc(s_oh, 1)
                wait(dve, s_oh, 5 * g + 4)
                dve.tensor_scalar(pick_c[:, :], pick[:, :], -1.0, None, ALU.min).then_inc(s_oh, 1)
                wait(dve, s_oh, 5 * g + 5)
                dve.tensor_tensor(onehot[:, :, :], expert_no[:, :, :],
                                  pick_c[:, :].unsqueeze(2).to_broadcast([P, GT, E]),
                                  ALU.is_equal).then_inc(s_ohr, 1)

            def slots_of(g):
                n = GT * E
                wait(dve, s_rank, g + 1)
                dve.tensor_copy(run_in[:, :, 0:1], run_out[:, :, GT:GT + 1]).then_inc(s_run, 1)
                dve.tensor_copy(run_in[:, :, 1:GT + 1],
                                ps_gate[:, 2 * n:3 * n].rearrange("p (e t) -> p e t", e=E)).then_inc(s_run, 1)
                wait(dve, s_run, 5 * g + 2)
                dve.tensor_tensor_scan(run_out[:, :, :].rearrange("p e t -> p (e t)"), run_mask[:, :],
                                       run_in[:, :, :].rearrange("p e t -> p (e t)"), 0.0, ALU.mult,
                                       ALU.add).then_inc(s_run, 1)
                wait(dve, s_run, 5 * g + 3)
                dve.tensor_tensor(slot_f[:, :, :], ps_gate[:, n:2 * n].rearrange("p (e t) -> p e t", e=E),
                                  run_out[:, :, 0:GT], ALU.add).then_inc(s_run, 1)
                wait(dve, s_run, 5 * g + 4)
                dve.tensor_tensor(slot_m[:, :, :], slot_f[:, :, :], onehot[:, :, :].rearrange("p t e -> p e t"),
                                  ALU.mult).then_inc(s_run, 1)
                wait(dve, s_run, 5 * g + 5)
                for k in range(2):
                    wait(dve, s_scat[k], 16 * CN * g)
                dve.tensor_reduce(slots[:, :], slot_m[:, :, :].rearrange("p e t -> p t e"), AX.X,
                                  ALU.add).then_inc(s_slot, 1)

            def chunk(c):
                here, k = c.within(NC), c.par
                q, s, a, o, y, r = c + 1, c + (-5), c + 4, c + (-1), c + (-2), c + (-3)
                if here:
                    wait(dve, s_SR, c.c + 1)
                    dve.scalar_tensor_tensor(out=Oar[:, k, :, 1:LP], in0=tq[:, k, :, 1:LP], scalar=1.0,
                                             in1=SRp[:, k, :, 1:LP], op0=ALU.add, op1=ALU.mult).then_inc(s_Oar, 1)
                    wait(dve, s_Oar, c.c + 1)
                    dve.scalar_tensor_tensor(out=Ep[:, k, :, 2:LP], in0=Oar[:, k, :, 1:L], scalar=-0.5,
                                             in1=hT[:, k, :, 2:LP], op0=ALU.mult, op1=ALU.add).then_inc(s_E, 1)
                if q.within(NC):
                    if q.fixed and q.c == 0:
                        dve.wait_ge(s_zero, 6)
                    wait(dve, s_K, q.c + 1)
                    dve.tensor_tensor_scan(Kc[:, q.par, :, :].rearrange("p s l -> p (s l)"), seq_mask[:, :],
                                           Kp[:, q.par, :, :].rearrange("p s l -> p (s l)"), 0.0,
                                           ALU.mult, ALU.add).then_inc(s_Kc, 1)
                if s.par == 0 and s.within(NC):
                    slots_of(s.half)
                if here:
                    wait(dve, s_E, c.c + 1)
                    dve.scalar_tensor_tensor(out=Ep[:, k, :, 2:LP], in0=t2[:, k, :, 1:L], scalar=1.0,
                                             in1=Ep[:, k, :, 2:LP], op0=ALU.add, op1=ALU.mult).then_inc(s_KE, 1)
                if q.within(NC):
                    wait(dve, s_KV, q.c + 1)
                    dve.tensor_tensor_scan(Sc[:, q.par, :, :].rearrange("p s l -> p (s l)"), seq_mask[:, :],
                                           KVp[:, q.par, :, :].rearrange("p s l -> p (s l)"), 0.0,
                                           ALU.mult, ALU.add).then_inc(s_Sc, 1)
                if here:
                    wait(dve, s_KE, c.c + 1)
                    dve.tensor_tensor_scan(S2[:, k, :, :].rearrange("p s l -> p (s l)"), seq_mask[:, :],
                                           Ep[:, k, :, :].rearrange("p s l -> p (s l)"), 0.0,
                                           ALU.mult, ALU.add).then_inc(s_S2, 1)
                if a.within(NC):
                    wait(dve, s_x[a.par], 16 * (a.half + 1))
                    stats(a, sA, x_in, 0)
                if here:
                    wait(dve, s_S2, c.c + 1)
                    dve.scalar_tensor_tensor(out=Mp[:, k, :, 2:LP], in0=tq[:, k, :, 1:L], scalar=1.0,
                                             in1=S2[:, k, :, 2:LP], op0=ALU.add, op1=ALU.mult).then_inc(s_M, 1)
                if o.within(NC):
                    wait(dve, s_proj, o.c + 1)
                    wait(dve, s_xr[o.par], 16 * (o.half + 1))
                    wait(dve, s_x1out[o.par], 16 * o.half)
                    wait(dve, sB["norm"], CN * (o.c - 1))
                    dve.tensor_tensor(x1_sb[:, o.par, :, :], ps_proj[:, :].rearrange("p (t d) -> p t d", t=CN),
                                      x_res[:, o.par, :, :], ALU.add).then_inc(s_x1, 1)
                if here:
                    wait(dve, s_M, c.c + 1)
                    wait(dve, s_proj, c.c - 1)
                    dve.scalar_tensor_tensor(out=Ot[:, k, :, :], in0=Mp[:, k, :, 1:LP], scalar=0.5 * KAPPA,
                                             in1=Oar[:, k, :, 1:LP], op0=ALU.mult, op1=ALU.add).then_inc(s_O, 1)
                    if c.fixed and c.c == 0:
                        dve.wait_ge(s_gin, 32)
                        dve.wait_ge(s_setup_act, 1)
                        dve.tensor_tensor(wg[:, :, :], wg[:, :, :], wT[:, 3:4, :].to_broadcast([P, B, D]),
                                          ALU.mult).then_inc(s_wg, 1)
                if a.within(NC):
                    means(a, sA, 0)
                if o.within(NC):
                    wait(dve, s_x1, o.c + 1)
                    stats(o, sB, x1_sb, 1)
                if y.within(NC):
                    wait(dve, sB["aggr"], CN * (y.c + 1))
                    wait(dve, s_rstd, y.c + 6)
                    wait(dve, s_zT, y.c - 1)
                    for t in range(CN):
                        dve.tensor_scalar(zz[:, y.par, t, :], x1_sb[:, y.par, t, :], mv[:, 1 - y.par, 1, t, 0:1],
                                          rstd[:, 1 - y.par, 1, t:t + 1], ALU.subtract, ALU.mult
                                          ).then_inc(sB["norm"], 1)
                if o.within(NC):
                    means(o, sB, 1)
                if r.par == 1 and r.within(NC):
                    if r.fixed and r.c == 1:
                        dve.wait_ge(s_iota, 9 + 2 * E + 1)
                    group_of(r.half)

            chunk(At(-4, -2, 0))
            chunk(At(-3, -2, 1))

            dve.wait_ge(s_th, 1)
            dve.scalar_tensor_tensor(out=cond_silu[:, :], in0=cond_th[:, :], scalar=1.0, in1=cond_sb[:, :],
                                     op0=ALU.add, op1=ALU.mult).then_inc(s_silu, 1)
            dve.wait_ge(s_setup_pe, 6)
            for n in range(4):
                dve.tensor_scalar(mod[:, n, :], ps_k2[:, n * B:(n + 1) * B], float(n % 2), None,
                                  ALU.add).then_inc(s_modw, 1)
            dve.wait_ge(s_modw, 4)
            dve.wait_ge(s_setup_pe, 7)
            g2 = ps_proj[0:B, 0:2 * D].rearrange("p (g d) -> p g d", g=2)
            dve.tensor_copy(gate_raw[:, :, :], g2).then_inc(s_gate, 1)
            dve.wait_ge(s_gate, 1)
            dve.tensor_scalar(gate_sign[:, :, :], gate_raw[:, :, :], 0.0, 2.0, ALU.is_ge, ALU.mult).then_inc(s_gate, 1)
            dve.scalar_tensor_tensor(out=gate_abs[:, :, :], in0=gate_raw[:, :, :], scalar=-1.0,
                                     in1=gate_raw[:, :, :], op0=ALU.mult, op1=ALU.max).then_inc(s_gate, 1)
            dve.wait_ge(s_gate, 3)
            dve.tensor_scalar(gate_abs[:, :, :], gate_abs[:, :, :], 0.25, None, ALU.max).then_inc(s_gabs, 1)
            dve.wait_ge(s_gabs, 1)
            dve.scalar_tensor_tensor(out=gates[:, 0:2, :], in0=gate_sign[:, :, :], scalar=-1.0,
                                     in1=gate_abs[:, :, :], op0=ALU.add, op1=ALU.mult).then_inc(s_gate, 1)
            dve.wait_ge(s_gate, 4)
            dve.wait_ge(s_small, 16 * 9)
            dve.tensor_tensor(gates[:, 2, :], gates[:, 0, :], bproj_bc[:, :], ALU.mult).then_inc(s_gate, 1)
            dve.wait_ge(s_gate, 5)
            dve.tensor_scalar(gates[:, 0, :], gates[:, 0, :], 0.5, None, ALU.mult).then_inc(s_gate, 1)
            walk(dve, -2, *A_SPAN[1:], chunk)

            dve.wait_ge(s_slot, NT // GT)
            step = [0]

            def then(ins):
                step[0] += 1
                ins.then_inc(s_plan, 1)
                dve.wait_ge(s_plan, step[0])

            dve.tensor_copy(end_i[:, :], run_out[:, :, GT]).then_inc(s_count, 1)
            then(dve.tensor_tensor(count_f[:, :], run_out[:, :, GT], region[:, 0:E], ALU.subtract))
            then(dve.tensor_scalar(count_i[:, :], count_f[:, :], float(FT - 1), None, ALU.add))
            then(dve.tensor_scalar(tiles_i[:, :], count_i[:, :], FT.bit_length() - 1, None, ALU.arith_shift_right))
            then(dve.tensor_copy(tiles_f[:, :], tiles_i[:, :]))
            then(dve.tensor_tensor_scan(tiles_end[:, :], run_mask[:, 1:E + 1], tiles_f[:, :], 0.0, ALU.mult, ALU.add))
            then(dve.scalar_tensor_tensor(out=shift[:, 1:E + 1], in0=tiles_end[:, :], scalar=-float(FT),
                                          in1=region[:, 1:E + 1], op0=ALU.mult, op1=ALU.add))
            then(dve.memset(shift[:, 0:1], 0.0))
            then(dve.tensor_tensor(past[:, :, :], tile_no[:, :].unsqueeze(2).to_broadcast([P, NJ, E]),
                                   tiles_end[:, :].unsqueeze(1).to_broadcast([P, NJ, E]), ALU.is_ge))
            then(dve.tensor_reduce(tile_e[:, :], past[:, :, :], AX.X, ALU.add))
            then(dve.tensor_scalar(tile_ec[:, :], tile_e[:, :], float(E - 1), None, ALU.min))
            dve.tensor_scalar(sel[:, :], tile_ec[0:E, :], part_no[0:E, :], None, ALU.is_equal).then_inc(s_planned, 1)
            for e in range(E + 1):
                dve.tensor_scalar(is_e[:, :, e], tile_e[:, :], float(e), None, ALU.is_equal).then_inc(s_ise, 1)
            dve.wait_ge(s_ise, E + 1)
            then(dve.tensor_tensor(is_e[:, :, :], is_e[:, :, :],
                                   shift[:, :].unsqueeze(1).to_broadcast([P, NJ, E + 1]), ALU.mult))
            then(dve.tensor_reduce(row_f[:, :], is_e[:, :, :], AX.X, ALU.add))
            then(dve.scalar_tensor_tensor(out=row_g[:, :], in0=tile_no[:, :], scalar=float(FT), in1=row_f[:, :],
                                          op0=ALU.mult, op1=ALU.add))
            then(dve.memset(plan[:, :, :], 0.0))
            then(dve.tensor_copy(plan[:, AHEAD:, 0], tile_ec[:, :]))
            dve.tensor_scalar(plan[:, 0:NJ, 1], row_g[:, :], float(E * RS), None, ALU.min).then_inc(s_planned, 1)
            dve.wait_ge(s_par, 1)

            def expert_tile(j):
                if j.within(NJ):
                    k = j.par
                    wait(dve, b_l1[1], j.c + 1)
                    wait(dve, b_y, j.c - 1)
                    for f in range(2):
                        a = dve.tensor_scalar(hid[:, k, 2 + f, :], ps_h[:, f * FT:(f + 1) * FT],
                                              par[:, 5 + f, bass.ds(j.c, 1)], 0.0, ALU.add, ALU.max)
                    a.then_inc(b_hidD, 1)
                u = j + (-1)
                if u.within(NJ):
                    k = u.par
                    wait(dve, b_up, u.c + 1)
                    wait(dve, s_uout[k], 16 * FS * u.half)
                    dve.tensor_tensor(u_sb[:, k, :, :], ps_k2[:, 0:FT].rearrange("p (s d) -> p s d", s=FS),
                                      rows_all[:, bass.ds(u.c, 1), :, 0:D].rearrange("p j s d -> p (j s) d"),
                                      ALU.add).then_inc(b_u, 1)
                z = j + 2
                if z.within(NJ):
                    k = z.par
                    wait(dve, b_rstd, z.c + 1)
                    wait(dve, b_zTp, z.c - 1)
                    for t in range(FS):
                        dve.tensor_scalar(bz[:, k, t, :], rows_all[:, bass.ds(z.c, 1), t, 0:D]
                                          .rearrange("p j d -> p (j d)"), bmv[:, k, t, 0:1], brstd[:, k, t:t + 1],
                                          ALU.subtract, ALU.mult).then_inc(b_z, 1)
                n = j + 3
                if n.within(NJ):
                    k = n.par
                    wait(dve, s_rin[k], 16 * (n.half + 1))
                    alone(dve)
                    for t in range(FS):
                        dve.bn_stats(bbn[:, k, t, :], rows_all[:, bass.ds(n.c, 1), t, 0:D]
                                     .rearrange("p j d -> p (j d)")).then_inc(b_bn, 1)
                    wait(dve, b_bn, FS * (n.c + 1))
                    wait(dve, b_z, FS * (n.c - 1))
                    alone(dve)
                    for t in range(FS):
                        dve.bn_aggr(bmv[:, k, t, :], bbn[:, k, t, :]).then_inc(b_aggr, 1)

            walk(dve, *B_SPAN, expert_tile)

            dve.wait_ge(s_gbin, 16)
            for g in range(NT // GT):
                dve.wait_ge(s_uin[g % 4], 32 * (g // 4 + 1))
                v = uc[:, g % 4, :, :].rearrange("p (b t) d -> p b t d", t=L // P)
                nb = GT * P // L
                for b in range(nb):
                    dve.tensor_tensor(v[:, b, :, :], v[:, b, :, :],
                                      gb_bc[:, g * nb + b:g * nb + b + 1, :].to_broadcast([P, L // P, D]),
                                      ALU.mult).then_inc(c_mul, 1)
                dve.wait_ge(c_mul, nb * (g + 1))
                xc = x1c[:, g % 4, :, :]
                dve.tensor_tensor(xc, xc, uc[:, g % 4, :, :], ALU.add).then_inc(c_add, 1)


_INS = ['L0_attn_x', 'L0_attn_Wq1', 'L0_attn_bq1', 'L0_attn_Wk1', 'L0_attn_bk1', 'L0_attn_Wk2', 'L0_attn_bk2',
        'L0_attn_Wproj', 'L0_attn_bproj', 'L0_ffn_centroids', 'L0_ffn_ln_g', 'L0_ffn_ln_b', 'L0_ffn_W1',
        'L0_ffn_b1', 'L0_ffn_W2', 'L0_ffn_b2', 'L0_c', 'L0_wmod']
_OUTS = [((32, 256, 128), 'float32')]


def kernel(**inputs):
    import numpy as _np
    import concourse.bacc as _bacc
    from concourse import mybir as _mybir
    from concourse.bass_utils import run_bass_kernel_spmd as _run

    nc = _bacc.Bacc("TRN2", target_bir_lowering=False, num_devices=1)
    arrays, args = {}, []
    for name in _INS:
        a = _np.ascontiguousarray(inputs[name])
        arrays[f"in_{name}_dram"] = a
        args.append(nc.dram_tensor(f"in_{name}_dram", a.shape, _mybir.dt.from_np(a.dtype), kind="ExternalInput").ap())
    for i, (shape, dtype) in enumerate(_OUTS):
        dt = _mybir.dt.from_np(_np.dtype(dtype))
        args.append(nc.dram_tensor(f"out_{i}_dram", shape, dt, kind="ExternalOutput").ap())
    build_block(nc, *args)
    r = _run(nc, [arrays], core_ids=[0])
    got = tuple(r.results[0][f"out_{i}_dram"] for i in range(len(_OUTS)))
    return got[0]
```

```python
from contextlib import ExitStack

import numpy as np

import concourse.bass as bass
from concourse import mybir


P = 128
F32 = mybir.dt.float32
BF16 = mybir.dt.bfloat16
I32 = mybir.dt.int32
ALU = mybir.AluOpType
ACT = mybir.ActivationFunctionType
AX = mybir.AxisListType
LN_EPS = 1e-5
CUM_EPS = 1e-6
MA_SLOPE = 0.02
MA_K = 0.02
LN_SCALE = 2.0 ** -44
LN_SHIFT = -44 * 0.6931471805599453


def build_block(nc, x, Wq1, bq1, Wk1, bk1, Wk2, bk2, Wproj, bproj, centroids, ln_g, ln_b,
                W1, b1, W2, b2, cond, wmod, out):
    B, L, D = x.shape
    E, _, F = W1.shape
    T = B * L
    NT = T // P
    CS = 2
    CT = CS * L
    CN = CT // P
    NC = T // CT
    GT = 2 * CN
    LP = L + 1
    FT = 2 * P
    FS = FT // P
    NJ = T // FT + E - 1
    FC = F // P
    RS = T + FT
    W = D + 1
    RW = W + 2 * D
    LAG = 4
    NV = 2 + FC
    ISQ = float(D) ** -0.5
    KAPPA = MA_SLOPE * ISQ
    assert D == P and NC % 2 == 0 and B == 32

    xt = x.rearrange("b l d -> (b l) d").rearrange("(t p) d -> p t d", p=P)
    out_rows = out.rearrange("b l d -> (b l) d")
    rows_dram = nc.dram_tensor("expert_rows", ((E + 1) * RS, RW), F32, kind="Internal").ap()
    gates_dram = nc.dram_tensor("gates_rows", (3, B, D), F32, kind="Internal").ap()

    with ExitStack() as ctx:
        def sb(name, shape, dt=F32):
            return ctx.enter_context(nc.sbuf_tensor(name, shape, dt))

        def sem(name):
            return ctx.enter_context(nc.semaphore(name))

        ctx.enter_context(nc.allow_non_contiguous_dma(reason="biases are loaded as columns"))
        ctx.enter_context(nc.allow_low_precision(reason="numbers of slots are whole and below 2^24"))

        bank = [ctx.enter_context(nc.psum_tensor(f"bank{i}", [P, 512], F32)) for i in range(8)]
        ps_x, ps_q, ps_k, ps_k2, ps_proj, ps_z, ps_h, ps_gate = bank

        ident = sb("ident", [P, P])
        lower = sb("lower", [P, P], BF16)
        ones_bf = sb("ones_bf", [P, P], BF16)
        ones_row = sb("ones_row", [1, P])
        expert_no = sb("expert_no", [P, GT, E])
        tile_no = sb("tile_no", [P, NJ])
        part_no = sb("part_no", [P, 1])
        part_i = sb("part_i", [P, 1], I32)
        iota_i = sb("iota_i", [P, GT, E], I32)
        iota_j = sb("iota_j", [P, NJ], I32)
        token_no = sb("token_no", [P, NT], I32)
        pad_rows = sb("pad_rows", [P, FS, RW])
        neg_half = sb("neg_half", [P, CN])
        seq_mask = sb("seq_mask", [P, CS * LP])
        run_mask = sb("run_mask", [P, E * (GT + 1)])
        w_raw = sb("w_raw", [P, 4, P])
        wT = sb("wT", [P, 4, P])
        bias_raw = sb("bias_raw", [P, 3])
        bias = sb("bias", [P, 3])
        cent_raw = sb("cent_raw", [E, D])
        centT = sb("centT", [P, E])
        cond_sb = sb("cond_sb", [B, D])
        cond_th = sb("cond_th", [B, D])
        cond_silu = sb("cond_silu", [B, D])
        condT = sb("condT", [P, B])
        wmod_sb = sb("wmod_sb", [P, 6 * D])
        mod = sb("mod", [P, 4, B])
        gate_raw = sb("gate_raw", [B, 2, D])
        gate_sign = sb("gate_sign", [B, 2, D])
        gate_abs = sb("gate_abs", [B, 2, D])
        gates = sb("gates", [B, 3, D])
        bproj_bc = sb("bproj_bc", [B, D])
        ga_in = sb("ga_in", [P, 2, CS, D])
        wg = sb("wg", [P, 2, CS, D])
        gbp_row = sb("gbp_row", [1, 2, CS, D])
        w1_all = sb("w1_all", [P, E, F])
        w2_all = sb("w2_all", [P, E, F])
        lnbias = sb("lnbias", [P, 1])
        epsv = sb("epsv", [P, 1])
        params = sb("params", [E, NV * D])

        x_in = sb("x_in", [P, 2, CN, D])
        x_res = sb("x_res", [P, 2, CN, D])
        x1_all = sb("x1_all", [P, NT, D])
        work = sb("work", [P, 13 * 2 * CS * LP])
        used = [0]

        def carve(shape):
            a, n = used[0], int(np.prod(shape))
            used[0] += n
            names = " ".join("abcd"[:len(shape)])
            return work[:, a:a + n].rearrange(f"p ({names}) -> p {names}", **dict(zip("abcd", shape)))

        xh = sb("xh", [P, 2, CN, D])
        hT = carve([2, CS, LP])
        Kp = carve([2, CS, LP])
        KVp = carve([2, CS, LP])
        tq = carve([2, CS, LP])
        t2 = carve([2, CS, LP])
        Kc = carve([2, CS, LP])
        lnK = carve([2, CS, LP])
        SRp = carve([2, CS, LP])
        Sc = carve([2, CS, LP])
        Oar = carve([2, CS, LP])
        Ep = carve([2, CS, LP])
        S2 = carve([2, CS, LP])
        Mp = carve([2, CS, LP])
        Ot = sb("Ot", [P, 2, CS, L])
        zz = sb("zz", [P, 2, CN, D])
        h2T = sb("h2T", [P, 2, CT])
        rows = sb("rows", [P, 2, CN, RW])
        bn = [sb(f"bn{i}", [P, 2, CN, 6]) for i in range(2)]
        mv = sb("mv", [P, 2, 2, CN, 2])
        lnv = sb("lnv", [P, 2, 2, CN])
        rstd = sb("rstd", [P, 2, 2, CN])
        negm = sb("negm", [P, 2, CN])
        top = sb("top", [P, GT])
        is_top = sb("is_top", [P, GT, E])
        pick = sb("pick", [P, GT])
        onehot = sb("onehot", [P, GT, E], BF16)
        run_in = sb("run_in", [P, E, GT + 1])
        run_out = sb("run_out", [P, E, GT + 1])
        slot_f = sb("slot_f", [P, E, GT])
        slot_m = sb("slot_m", [P, E, GT])
        slots = sb("slots", [P, GT], I32)
        count_f = sb("count_f", [P, E])
        region = sb("region", [P, E + 1])
        count_i = sb("count_i", [P, E], I32)
        end_i = sb("end_i", [P, E], I32)
        tiles_i = sb("tiles_i", [P, E], I32)
        tiles_f = sb("tiles_f", [P, E])
        tiles_end = sb("tiles_end", [P, E])
        shift = sb("shift", [P, E + 1])
        past = sb("past", [P, NJ, E])
        tile_e = sb("tile_e", [P, NJ])
        tile_ec = sb("tile_ec", [P, NJ])
        is_e = sb("is_e", [P, NJ, E + 1])
        row_f = sb("row_f", [P, NJ])
        row_g = sb("row_g", [P, NJ])
        plan = sb("plan", [P, NJ, 2], I32)
        sel = sb("sel", [E, NJ])
        par = sb("par", [P, NV, NJ])
        used[0] = 0
        b2_bc = carve([E, D])
        w1_sb = carve([2, F])
        rin = carve([2, FS, D])
        bbn = sb("bbn", [P, 2, FS, 6])
        bmv = sb("bmv", [P, 2, FS, 2])
        bveps = sb("bveps", [P, 2, FS])
        brstd = sb("brstd", [P, 2, FS])
        bz = carve([2, FS, D])
        zT = carve([2, FT])
        hid = carve([2, FC, FT])
        u_sb = carve([2, FS, D])
        ids = sb("ids", [P, 2, FS], I32)
        full = carve([2, FS, RW])

        s_w = sem("weights_in"); s_small = sem("small_in"); s_params = sem("params_in"); s_cent_in = sem("centroids_in"); s_centp = sem("centT_psum"); s_cent = sem("centT_ready"); s_cond = sem("cond_in"); s_mod_in = sem("mod_in")
        s_x = [sem(f"x_in{i}") for i in range(2)]
        s_xr = [sem(f"x_res{i}") for i in range(2)]
        s_fill = [sem(f"rows_filled{i}") for i in range(2)]
        s_const = sem("constants"); s_ident = sem("ident_ready"); s_iota = sem("iota_ready")
        s_pads = sem("pads_ready"); s_zero = sem("leading_columns")
        s_setup_pe = sem("setup_pe"); s_setup_act = sem("setup_act"); s_modw = sem("mod_ready"); s_lnb = sem("ln_shift_ready")
        s_th = sem("cond_tanh"); s_silu = sem("cond_silu"); s_gate = sem("gate_steps"); s_gabs = sem("gate_abs"); s_ise = sem("is_expert"); s_tok = sem("token_numbers")
        s_gout = sem("gates_out"); s_ga = [sem(f"ga_in{i}") for i in range(2)]; s_gbp = [sem(f"gbp_in{i}") for i in range(2)]; s_wg = sem("wg_ready")
        sA = {n: sem("x_" + n) for n in ("bn", "aggr", "norm")}
        sB = {n: sem("z_" + n) for n in ("bn", "aggr", "norm")}
        s_lnv = sem("ln_var_ready"); s_rstd = sem("rstd_ready"); s_negm = sem("neg_mean_ready")
        s_xT = sem("xT_psum"); s_hT = sem("hT_ready"); s_qkv = sem("qkv_psum")
        s_tq = sem("tq_ready"); s_t2 = sem("t2_ready"); s_K = sem("K_ready"); s_KV = sem("KV_ready")
        s_Kc = sem("Kc_ready"); s_Sc = sem("Sc_ready"); s_ln = sem("lnK_ready"); s_R = sem("R_ready")
        s_SR = sem("SR_ready"); s_Oar = sem("Oar_ready"); s_E = sem("E_ready"); s_KE = sem("KE_ready")
        s_S2 = sem("S2_ready"); s_M = sem("M_ready"); s_O = sem("O_ready")
        s_proj = sem("proj_psum"); s_x1 = sem("x1_ready")
        s_zT = sem("zT_psum"); s_h2T = sem("h2T_ready"); s_h2 = sem("h2_psum"); s_row = sem("rows_ready")
        s_gates = sem("logits_psum"); s_oh = sem("onehot_steps"); s_ohr = sem("onehot_ready")
        s_rank = sem("rank_psum"); s_run = sem("run_steps"); s_slot = sem("slots_ready")
        s_scat = [sem(f"rows_scattered{i}") for i in range(2)]
        s_plan = sem("plan_steps"); s_planned = sem("plan_ready"); s_sel = sem("params_psum")
        s_par = sem("params_ready"); s_count = sem("counts_ready"); s_pad_out = sem("pads_out")
        s_rin = [sem(f"rows_in{i}") for i in range(2)]
        s_experts = sem("experts_in")
        b_bn = sem("b_bn"); b_aggr = sem("b_aggr"); b_veps = sem("b_veps"); b_rstd = sem("b_rstd")
        b_z = sem("b_z"); b_zTp = sem("b_zT_psum"); b_zT = sem("b_zT_ready")
        b_w1 = sem("b_W1_ready"); b_l1 = sem("b_hidden_psum")
        b_hidA = sem("b_hidden_act"); b_hidD = sem("b_hidden_dve")
        b_y = sem("b_y_psum"); b_bias = sem("b_bias_added"); b_sum = sem("b_sum_ready"); b_gated = sem("b_gated"); b_u = sem("b_u_ready")
        b_ids = sem("b_ids_ready")
        s_uout = [sem(f"u_out{i}") for i in range(2)]
        s_full = [sem(f"full_rows_in{i}") for i in range(2)]

        def alone(eng):
            eng.sem_inc(s_met[eng], 1)

        def wait(eng, s, value):
            if isinstance(value, int) and value <= 0:
                return
            eng.wait_ge(s, value)

        def expert_of(eng, j):
            return eng.value_load(plan[0:1, bass.ds(j.c, 1), 0:1].rearrange("p o w -> p (o w)"),
                                  min_val=0, max_val=E - 1)

        def of_expert(table, e, lo, hi):
            return table[:, bass.ds(e, 1), lo:hi].rearrange("p o d -> p (o d)")

        def write_pads(eng, experts):
            for e in experts:
                end = eng.value_load(end_i[0:1, e:e + 1], min_val=e * RS, max_val=e * RS + T)
                eng.dma_start(rows_dram[bass.ds(end, FT), :].rearrange("(s p) w -> p s w", p=P),
                              pad_rows[:, :, :]).then_inc(s_pad_out, 16)

        class At:

            def __init__(self, c, half, par):
                self.c, self.half, self.par = c, half, par
                self.fixed = isinstance(c, int)

            def __add__(self, o):
                k = self.par + o
                return At(self.c + o, self.half + k // 2, k % 2)

            def within(self, n):
                return not self.fixed or 0 <= self.c < n

        def walk(eng, first, lo, hi, last, body, unroll=2):
            for c in range(first, lo):
                body(At(c, c // 2, c % 2))
            with eng.Fori(lo // unroll, hi // unroll) as i:
                rest = lo % unroll
                at = At(i * unroll + rest, i * (unroll // 2) + rest // 2, rest % 2)
                for step in range(unroll):
                    body(at + step if step else at)
            for c in range(hi, last):
                body(At(c, c // 2, c % 2))

        A_SPAN = (-4, 7, 11, NC + 5)
        B_SPAN = (-3, 4, 36, NJ + 2)

        s_met = {eng: sem(f"met_{n}") for n, eng in (("pool", nc.gpsimd), ("dve", nc.vector), ("sp", nc.sync))}
        block = ctx.enter_context(nc.Block())

        @block.sync
        def _(sp):
            for k in range(2):
                sp.dma_start(x_in[:, k, :, :], xt[:, k * CN:(k + 1) * CN, :]).then_inc(s_x[k], 16)
            for n, w in enumerate((Wq1, Wk1, Wk2, Wproj)):
                sp.dma_start(w_raw[:, n, :], w).then_inc(s_w, 16)
            for n, v in enumerate((bq1, bk2, bk1)):
                sp.dma_start(bias_raw[:, n:n + 1], v.rearrange("(p o) -> p o", o=1)).then_inc(s_small, 16)
            sp.dma_start(bproj_bc[:, :], bproj.partition_broadcast(B)).then_inc(s_small, 16)
            sp.dma_start(cent_raw[:, :], centroids).then_inc(s_cent_in, 16)
            weights = [(w1_all[:, e:e + 2, :], W1[e:e + 2].rearrange("e d f -> d e f")) for e in range(0, E, 2)]
            weights += [(w2_all[:, :, f * D:(f + 1) * D], W2[:, f * P:(f + 1) * P, :].rearrange("e p d -> p e d"))
                        for f in range(FC)]

            def gates_of(c, which, n):
                return (gates_dram[which, bass.ds(c * CS, CS), :].rearrange("s d -> (s d)").partition_broadcast(n)
                        .rearrange("p (s d) -> p s d", s=CS))

            def stream(c):
                q = c + 1
                if q.within(NC):
                    k = q.par
                    wait(sp, s_proj, q.c - 1)
                    alone(sp)
                    wait(sp, s_wg, q.c - 1)
                    alone(sp)
                    wait(sp, s_ga[k], 16 * q.half)
                    alone(sp)
                    sp.dma_start(ga_in[:, k, :, :], gates_of(q.c, 0, P)).then_inc(s_ga[k], 16)
                    wait(sp, s_gbp[k], 16 * q.half)
                    alone(sp)
                    sp.dma_start(gbp_row[:, k, :, :], gates_of(q.c, 2, 1)).then_inc(s_gbp[k], 16)
                if c.fixed and 0 <= c.c < NC:
                    sp.dma_start(*weights.pop()).then_inc(s_experts, 16)
                m = c + 5
                if m.within(NC):
                    wait(sp, sA["norm"], CN * (m.c - 1))
                    alone(sp)
                    wait(sp, s_x[m.par], 16 * m.half)
                    alone(sp)
                    sp.dma_start(x_in[:, m.par, :, :], xt[:, bass.ds(m.c * CN, CN), :]).then_inc(s_x[m.par], 16)
                n = c + 1
                if n.within(NC):
                    wait(sp, s_x1, n.c - 1)
                    alone(sp)
                    wait(sp, s_xr[n.par], 16 * n.half)
                    alone(sp)
                    sp.dma_start(x_res[:, n.par, :, :], xt[:, bass.ds(n.c * CN, CN), :]).then_inc(s_xr[n.par], 16)
                if c.fixed and c.c == NC + 1:
                    sp.wait_ge(s_proj, NC)
                    sp.dma_start(b2_bc[:, :, :].rearrange("p e d -> p (e d)"),
                                 b2.rearrange("e d -> (e d)").partition_broadcast(P)).then_inc(s_experts, 16)
                z = c + (-3)
                if z.within(NC):
                    k = z.par
                    wait(sp, s_x1, z.c + 1)
                    alone(sp)
                    wait(sp, s_scat[k], 16 * CN * z.half)
                    alone(sp)
                    sp.dma_start(rows[:, k, :, W:W + D], x1_all[:, bass.ds(z.c * CN, CN), :]).then_inc(s_fill[k], 16)
                    for t in range(L // P):
                        sp.dma_start(rows[:, k, :, W + D:RW].rearrange("p (s t) d -> p s t d", s=CS)[:, :, t, :],
                                     gates_of(z.c, 1, P)).then_inc(s_fill[k], 16)

            stream(At(-3, -2, 1))
            sp.wait_ge(s_gate, 6)
            sp.dma_start(gates_dram.rearrange("g b d -> b g d"), gates[:, :, :]).then_inc(s_gout, 16)
            sp.wait_ge(s_gout, 16)

            walk(sp, -2, 3, 11, NC + 3, stream)
            assert not weights

            sp.wait_ge(s_pads, 2)
            sp.dma_start(rows_dram[E * RS:E * RS + FT, :].rearrange("(s p) w -> p s w", p=P),
                         pad_rows[:, :, :]).then_inc(s_pad_out, 16)
            sp.wait_ge(s_count, 1)
            write_pads(sp, range(0, E, 2))
            sp.wait_ge(s_pad_out, 16 * (E + 1))
            for k in range(2):
                sp.wait_ge(s_scat[k], 16 * NT // 2)

            sp.wait_ge(s_planned, 2)

            def first_row(j):
                return sp.value_load(plan[0:1, bass.ds(j.c, 1), 1:2].rearrange("p o w -> p (o w)"),
                                     min_val=0, max_val=E * RS)

            def load_tile(m):
                if m.within(NJ):
                    r = first_row(m)
                    wait(sp, b_z, FS * (m.c - 1))
                    alone(sp)
                    wait(sp, s_rin[m.par], 16 * m.half)
                    alone(sp)
                    sp.dma_start(rin[:, m.par, :, :], rows_dram[bass.ds(r, FT), 0:D]
                                 .rearrange("(s p) w -> p s w", p=P)).then_inc(s_rin[m.par], 16)
                u = m + (-LAG)
                if u.within(NJ):
                    r = first_row(u)
                    wait(sp, b_u, u.c - 1)
                    alone(sp)
                    wait(sp, b_ids, u.c - 1)
                    alone(sp)
                    sp.dma_start(full[:, u.par, :, :], rows_dram[bass.ds(r, FT), :]
                                 .rearrange("(s p) w -> p s w", p=P)).then_inc(s_full[u.par], 16)

            walk(sp, 0, 6, 38, NJ + LAG, load_tile, 4)
            for k in range(2):
                sp.wait_ge(s_uout[k], 16 * FS * ((NJ + 1 - k) // 2))

        @block.gpsimd
        def _(pool):
            pool.memset(ident[:, :], 0.0).then_inc(s_ident, 1)
            pool.wait_ge(s_ident, 1)
            pool.affine_select(out=ident[:, :], in_=ident[:, :], compare_op=ALU.not_equal, fill=1.0,
                               base=0, pattern=[[-1, P]], channel_multiplier=1).then_inc(s_ident, 1)
            pool.memset(neg_half[:, :], -0.5).then_inc(s_const, 1)
            pool.memset(ones_row[:, :], 1.0).then_inc(s_const, 1)
            pool.memset(ones_bf[:, :], 1.0).then_inc(s_const, 1)
            pool.memset(lower[:, :], 1.0).then_inc(s_const, 1)
            pool.wait_ge(s_const, 4)
            pool.affine_select(out=lower[:, :], in_=lower[:, :], compare_op=ALU.is_gt, fill=0.0,
                               base=0, pattern=[[1, P]], channel_multiplier=-1).then_inc(s_const, 1)

            def number_rows(c, g, first):
                wait(pool, s_scat[first], 16 * CN * g)
                alone(pool)
                pool.tensor_copy(rows[:, first, :, D:W].bitcast(I32),
                                 token_no[:, bass.ds(c * CN, CN)].unsqueeze(2)).then_inc(s_tok, 1)
                wait(pool, s_tok, c + 1)
                wait(pool, s_row, c + 1)
                wait(pool, s_fill[first], 16 * (1 + L // P) * (g + 1))
                wait(pool, s_slot, g + 1)
                alone(pool)

            def chunk(c):
                s = c + (-5)
                if s.within(NC):
                    if s.fixed and s.c == 0:
                        pool.wait_ge(s_iota, 1)
                    number_rows(s.c, s.half, s.par)
                    for t in range(CN):
                        pool.indirect_dma_start(rows_dram, bass.IndirectOffsetOnAxis(
                            ap=slots[:, s.par * CN + t:s.par * CN + t + 1], axis=0),
                            rows[:, s.par, t, :], None).then_inc(s_scat[s.par], 16)
                q = c + 1
                if q.within(NC):
                    k = q.par
                    wait(pool, s_R, q.c + 1)
                    wait(pool, s_Sc, q.c + 1)
                    pool.tensor_tensor(SRp[:, k, :, 1:LP], Sc[:, k, :, 1:LP], lnK[:, k, :, 1:LP],
                                       ALU.mult).then_inc(s_SR, 1)
                a = c + 3
                if a.within(NC):
                    k = a.par
                    wait(pool, sA["aggr"], CN * (a.c + 1))
                    alone(pool)
                    pool.tensor_scalar(negm[:, k, :], mv[:, k, 0, :, 0], -1.0, 0.0, ALU.mult,
                                       ALU.add).then_inc(s_negm, 1)
                    wait(pool, s_xT, a.c - 1)
                    wait(pool, s_rstd, a.c + 1)
                    wait(pool, s_negm, a.c + 1)
                    alone(pool)
                    for t in range(CN):
                        pool.tensor_scalar(xh[:, k, t, :], x_in[:, k, t, :], negm[:, k, t:t + 1],
                                           rstd[:, k, 0, t:t + 1], ALU.add, ALU.mult).then_inc(sA["norm"], 1)
                if q.within(NC):
                    k = q.par
                    if q.fixed and q.c == 0:
                        pool.wait_ge(s_setup_act, 2)
                    wait(pool, s_ga[k], 16 * (q.half + 1))
                    wait(pool, s_proj, q.c - 1)
                    pool.tensor_tensor(wg[:, k, :, :], ga_in[:, k, :, :],
                                       wT[:, 3:4, :].to_broadcast([P, CS, D]), ALU.mult).then_inc(s_wg, 1)
                n = c + 2
                if n.within(NC):
                    k = n.par
                    wait(pool, s_hT, 2 * (n.c + 1))
                    wait(pool, s_K, n.c + 1)
                    if n.fixed and n.c == 0:
                        pool.wait_ge(s_zero, 6)
                    pool.tensor_tensor(KVp[:, k, :, 1:LP], Kp[:, k, :, 1:LP], hT[:, k, :, 1:LP],
                                       ALU.mult).then_inc(s_KV, 1)

            pool.iota(token_no[:, :], pattern=[[P, NT]], base=0, channel_multiplier=1).then_inc(s_iota, 1)
            pool.iota(iota_i[:, :, :], pattern=[[0, GT], [1, E]], base=-E, channel_multiplier=0).then_inc(s_iota, 1)
            pool.iota(iota_j[:, :], pattern=[[1, NJ]], base=0, channel_multiplier=0).then_inc(s_iota, 1)
            pool.iota(part_i[:, :], pattern=[[0, 1]], base=0, channel_multiplier=1).then_inc(s_iota, 1)
            pool.memset(pad_rows[:, :, :], 0.0).then_inc(s_pads, 1)
            pool.wait_ge(s_pads, 1)
            pool.memset(pad_rows[:, :, D:W].bitcast(I32), T).then_inc(s_pads, 1)
            pool.memset(run_mask[:, :], 1.0).then_inc(s_iota, 1)
            pool.wait_ge(s_iota, 5)
            pool.tensor_copy(expert_no[:, :, :], iota_i[:, :, :]).then_inc(s_iota, 1)
            pool.tensor_copy(tile_no[:, :], iota_j[:, :]).then_inc(s_iota, 1)
            pool.tensor_copy(part_no[:, :], part_i[:, :]).then_inc(s_iota, 1)
            pool.memset(run_mask[:, :].rearrange("p (e t) -> p e t", e=E)[:, :, 0:1], 0.0).then_inc(s_iota, 1)
            for e in range(E):
                pool.memset(run_out[:, e, GT:GT + 1], float(e * RS)).then_inc(s_iota, 1)
            for e in range(E + 1):
                pool.memset(region[:, e:e + 1], float(e * RS)).then_inc(s_iota, 1)
            walk(pool, *A_SPAN, chunk)

            def expert_step(j):
                n = j + 3
                if n.within(NJ):
                    k = n.par
                    wait(pool, b_aggr, FS * (n.c + 1))
                    alone(pool)
                    pool.tensor_scalar(bveps[:, k, :], bmv[:, k, :, 1], LN_EPS, None, ALU.add).then_inc(b_veps, 1)
                    wait(pool, b_veps, n.c + 1)
                    wait(pool, b_z, FS * (n.c - 1))
                    pool.tensor_tensor(brstd[:, k, :], bveps[:, k, :], neg_half[:, 0:FS], ALU.pow).then_inc(b_rstd, 1)
                u = j + (-2)
                if u.within(NJ):
                    k = u.par
                    wait(pool, s_uout[k], 16 * FS * u.half)
                    alone(pool)
                    wait(pool, s_full[k], 16 * (u.half + 1))
                    alone(pool)
                    pool.tensor_copy(ids[:, k, :], full[:, k, :, D:W].bitcast(I32)
                                     .rearrange("p s w -> p (s w)")).then_inc(b_ids, 1)
                    wait(pool, b_ids, u.c + 1)
                    wait(pool, b_u, u.c + 1)
                    alone(pool)
                    for t in range(FS):
                        pool.indirect_dma_start(out_rows, bass.IndirectOffsetOnAxis(ap=ids[:, k, t:t + 1], axis=0),
                                                u_sb[:, k, t, :], None, bounds_check=T - 1,
                                                oob_is_err=False).then_inc(s_uout[k], 16)

            walk(pool, *B_SPAN, expert_step, 4)

        @block.tensor
        def _(pe):
            pe.wait_ge(s_ident, 2)
            pe.wait_ge(s_silu, 1)
            pe.transpose(ps_k[:, 0:B], cond_silu[:, :], ident[0:B, 0:B]).then_inc(s_setup_pe, 1)
            pe.wait_ge(s_setup_act, 1)
            pe.wait_ge(s_mod_in, 16)
            for n, part in enumerate((0, 1, 3, 4)):
                mm = pe.matmul(ps_k2[:, n * B:(n + 1) * B], wmod_sb[:, part * D:(part + 1) * D], condT[:, :],
                               start=True, stop=True)
            mm.then_inc(s_setup_pe, 1)
            for n, part in enumerate((2, 5)):
                mm = pe.matmul(ps_proj[0:B, n * D:(n + 1) * D], condT[:, :], wmod_sb[:, part * D:(part + 1) * D],
                               start=True, stop=True)
            mm.then_inc(s_setup_pe, 1)
            pe.wait_ge(s_w, 64)
            for n in range(4):
                pe.transpose(ps_q[:, n * P:(n + 1) * P], w_raw[:, n, :], ident[:, :]).then_inc(s_setup_pe, 1)

            def ranks(g):
                wait(pe, s_ohr, g + 1)
                oh = onehot[:, :, :].rearrange("p t e -> p e t")
                pe.matmul(ps_gate[:, GT * E:2 * GT * E].rearrange("p (e t) -> p e t", e=E), lower[:, :], oh,
                          start=True, stop=True)
                pe.matmul(ps_gate[:, 2 * GT * E:3 * GT * E].rearrange("p (e t) -> p e t", e=E), ones_bf[:, :], oh,
                          start=True, stop=True).then_inc(s_rank, 1)

            def rows_back(z):
                wait(pe, s_row, z.c)
                for t in range(CN):
                    mm = pe.transpose(ps_h[:, t * P:(t + 1) * P], h2T[:, z.par, t * P:(t + 1) * P], ident[:, :])
                mm.then_inc(s_h2, 1)

            def chunk(c):
                z = c + (-3)
                if z.within(NC):
                    k = z.par
                    wait(pe, sB["norm"], CN * (z.c + 1))
                    wait(pe, s_h2T, 2 * z.c)
                    for t in range(CN):
                        mm = pe.transpose(ps_z[:, t * P:(t + 1) * P], zz[:, k, t, :], ident[:, :])
                    mm.then_inc(s_zT, 1)
                g = c + (-5)
                if g.par == 0 and g.within(NC):
                    if g.fixed and g.c == 0:
                        pe.wait_ge(s_const, 5)
                    ranks(g.half)
                n = c + 2
                if n.within(NC):
                    wait(pe, sA["norm"], CN * (n.c + 1))
                    wait(pe, s_hT, 2 * n.c)
                    for t in range(CN):
                        mm = pe.transpose(ps_x[:, t * P:(t + 1) * P], xh[:, n.par, t, :], ident[:, :])
                    mm.then_inc(s_xT, 1)
                o = c + (-1)
                if o.within(NC):
                    wait(pe, s_wg, o.c + 1)
                    wait(pe, s_gbp[o.par], 16 * (o.half + 1))
                    wait(pe, s_O, o.c + 1)
                    wait(pe, s_x1, o.c)
                    for t in range(CN):
                        s = t * P // L
                        dst = ps_proj[:, t * P:(t + 1) * P]
                        pe.matmul(dst, Ot[:, o.par, s, (t * P) % L:(t * P) % L + P],
                                  wg[:, o.par, s, :], start=True, stop=False)
                        mm = pe.matmul(dst, ones_row[:, :], gbp_row[:, o.par, s, :], start=False, stop=True)
                    mm.then_inc(s_proj, 1)
                if z.within(NC):
                    wait(pe, s_h2T, 2 * (z.c + 1))
                    if z.fixed and z.c == 0:
                        pe.wait_ge(s_cent, 1)
                    if k == 0:
                        wait(pe, s_slot, z.half)
                    for t in range(CN):
                        at = (k * CN + t) * E
                        mm = pe.matmul(ps_gate[:, at:at + E], h2T[:, k, t * P:(t + 1) * P], centT[:, :],
                                       start=True, stop=True)
                    mm.then_inc(s_gates, 1)
                if c.fixed and c.c == 0:
                    pe.wait_ge(s_cent_in, 16)
                    pe.transpose(ps_gate[:, 0:E], cent_raw[:, :], ident[0:E, 0:E]).then_inc(s_centp, 1)
                if n.within(NC):
                    wait(pe, s_hT, 2 * (n.c + 1))
                    if n.fixed and n.c == 0:
                        pe.wait_ge(s_setup_act, 2)
                        pe.wait_ge(s_modw, 4)
                        pe.wait_ge(s_gate, 1)
                    for m, (dst, free) in enumerate(((ps_k, s_K), (ps_q, s_tq), (ps_k2, s_t2))):
                        wait(pe, free, n.c)
                        pe.matmul(dst[:, :], wT[:, (1, 0, 2)[m], :], hT[:, n.par, :, 1:LP],
                                  start=True, stop=True).then_inc(s_qkv, 1)
                if z.within(NC) and (not z.fixed or z.c < NC - 1):
                    rows_back(z)
                if c.fixed and c.c == NC + 3:
                    rows_back(c + (-4))

            walk(pe, *A_SPAN, chunk)

            pe.wait_ge(s_planned, 1)
            pe.wait_ge(s_params, 48)
            for n in range(NV):
                mm = pe.matmul(ps_x[:, n * NJ:(n + 1) * NJ], params[:, n * D:(n + 1) * D], sel[:, :],
                               start=True, stop=True)
            mm.then_inc(s_sel, 1)

            for s in (s_x1, s_row, s_K, s_tq, s_t2):
                pe.wait_ge(s, NC)
            pe.wait_ge(s_h2T, 2 * NC)
            pe.wait_ge(s_planned, 2)
            pe.wait_ge(s_experts, 16 * (E // 2 + FC + 1))

            def expert_tile(j):
                o = j + (-1)
                if o.within(NJ):
                    e = expert_of(pe, o)
                if j.within(NJ):
                    k = j.par
                    wait(pe, b_zT, j.c + 1)
                    wait(pe, b_w1, j.c + 1)
                    for f in range(FC):
                        if f == 0:
                            wait(pe, b_hidA, j.c)
                        if f == FC - 1:
                            wait(pe, b_hidD, j.c)
                        dst = (ps_proj[:, 0:FT], ps_proj[:, FT:2 * FT], ps_h[:, 0:FT], ps_k2[:, 0:FT])[f]
                        pe.matmul(dst, w1_sb[:, k, f * P:(f + 1) * P], zT[:, k, :], start=True, stop=True
                                  ).then_inc(b_l1, 1)
                n = j + 1
                if n.within(NJ):
                    wait(pe, b_z, FS * (n.c + 1))
                    wait(pe, b_zT, n.c)
                    for t in range(FS):
                        mm = pe.transpose(ps_z[:, t * P:(t + 1) * P], bz[:, n.par, t, :], ident[:, :])
                    mm.then_inc(b_zTp, 1)
                if o.within(NJ):
                    k = o.par
                    wait(pe, b_bias, o.c - 1)
                    for t in range(FS):
                        for f in range(FC):
                            if t == 0 and f == 0:
                                wait(pe, b_hidA, o.c + 1)
                            if t == 0 and f == FC - 1:
                                wait(pe, b_hidD, o.c + 1)
                            mm = pe.matmul((ps_q, ps_k)[k][:, t * D:(t + 1) * D], hid[:, k, f, t * P:(t + 1) * P],
                                           of_expert(w2_all, e, f * D, (f + 1) * D),
                                           start=(f == 0), stop=(f == FC - 1))
                    mm.then_inc(b_y, 1)

            walk(pe, *B_SPAN, expert_tile, 4)

        @block.scalar
        def _(act):
            act.dma_start(cond_sb[:, :], cond).then_inc(s_cond, 16)
            act.dma_start(wmod_sb[:, :], wmod).then_inc(s_mod_in, 16)
            def row_copy(z):
                wait(act, s_h2, z.c + 1)
                wait(act, s_scat[z.par], 16 * CN * z.half)
                act.activation(rows[:, z.par, :, 0:D], ps_h[:, :].rearrange("p (t d) -> p t d", t=CN),
                               ACT.Copy).then_inc(s_row, 1)

            def second_norm(c):
                z = c + (-3)
                if z.within(NC):
                    k = z.par
                    wait(act, s_zT, z.c + 1)
                    wait(act, s_gates, z.c - 1)
                    for s in range(CS):
                        act.activation(h2T[:, k, s * L:(s + 1) * L], ps_z[:, s * L:(s + 1) * L], ACT.Identity,
                                       bias=mod[:, 2, bass.ds(z.c * CS + s, 1)],
                                       scale=mod[:, 3, bass.ds(z.c * CS + s, 1)]).then_inc(s_h2T, 1)

            def chunk(c):
                z = c + (-3)
                last = c.fixed and c.c > NC
                if not last:
                    second_norm(c)
                n = c + 2
                if n.within(NC):
                    if n.fixed and n.c == 0:
                        act.wait_ge(s_modw, 4)
                    wait(act, s_xT, n.c + 1)
                    wait(act, s_E, n.c - 1)
                    for s in range(CS):
                        act.activation(hT[:, n.par, s, 1:LP], ps_x[:, s * L:(s + 1) * L], ACT.Identity,
                                       bias=mod[:, 0, bass.ds(n.c * CS + s, 1)],
                                       scale=mod[:, 1, bass.ds(n.c * CS + s, 1)]).then_inc(s_hT, 1)
                q = c + 1
                k = q.par
                a, y = c + 3, c + (-2)
                kinds = slice(0 if a.within(NC) else 1, 2 if y.within(NC) else 1)
                if q.within(NC):
                    wait(act, s_Kc, q.c + 1)
                    act.activation(lnK[:, k, :, :], Kc[:, k, :, :], ACT.Ln, scale=LN_SCALE).then_inc(s_ln, 1)
                if a.within(NC) or y.within(NC):
                    if c.fixed and c.c == -3:
                        act.wait_ge(s_lnb, 2)
                    if a.within(NC):
                        wait(act, sA["aggr"], CN * (a.c + 1))
                        wait(act, sA["norm"], CN * (a.c - 1))
                    if y.within(NC):
                        wait(act, sB["aggr"], CN * (y.c + 1))
                        wait(act, sB["norm"], CN * (y.c - 1))
                    act.activation(lnv[:, k, kinds, :], mv[:, k, kinds, :, 1], ACT.Ln, bias=epsv[:, :]
                                   ).then_inc(s_lnv, 1)
                if q.within(NC):
                    wait(act, s_ln, q.c + 1)
                    act.activation(lnK[:, k, :, :], lnK[:, k, :, :], ACT.Exp, scale=-1.0,
                                   bias=lnbias[:, :]).then_inc(s_R, 1)
                if a.within(NC) or y.within(NC):
                    wait(act, s_lnv, c.c + 4)
                    act.activation(rstd[:, k, kinds, :], lnv[:, k, kinds, :], ACT.Exp, scale=-0.5
                                   ).then_inc(s_rstd, 1)
                if last:
                    second_norm(c)
                if n.fixed and n.c == 0:
                    act.wait_ge(s_small, 16 * 4)
                    act.mul(bias[:, 0:1], bias_raw[:, 0:1], 0.5).then_inc(s_setup_act, 1)
                    act.mul(bias[:, 1:2], bias_raw[:, 1:2], 0.5 * MA_K * ISQ).then_inc(s_setup_act, 1)
                    act.copy(bias[:, 2:3], bias_raw[:, 2:3]).then_inc(s_setup_act, 1)
                    act.wait_ge(s_setup_act, 5)
                if c.fixed and c.c == 0:
                    act.wait_ge(s_centp, 1)
                    act.activation(centT[:, :], ps_gate[:, 0:E], ACT.Copy).then_inc(s_cent, 1)
                    act.dma_start(params[:, 0:D], ln_g).then_inc(s_params, 16)
                    act.dma_start(params[:, D:2 * D], ln_b).then_inc(s_params, 16)
                    act.dma_start(params[:, 2 * D:NV * D], b1).then_inc(s_params, 16)
                if n.within(NC):
                    for m, (src, dst, f, b, scale, done) in enumerate((
                            (ps_k, Kp, ACT.Exp, 2, 1.0, s_K), (ps_q, tq, ACT.Tanh, 0, 0.5, s_tq),
                            (ps_k2, t2, ACT.Tanh, 1, 0.5 * MA_K * ISQ, s_t2))):
                        wait(act, s_qkv, 3 * n.c + m + 1)
                        if m == 1:
                            wait(act, s_M, n.c - 1)
                        if n.fixed and n.c == 0 and m == 0:
                            act.wait_ge(s_zero, 6)
                        act.activation(dst[:, n.par, :, 1:LP], src[:, :].rearrange("p (s l) -> p s l", s=CS), f,
                                       bias=bias[:, b:b + 1], scale=scale).then_inc(done, 1)
                if z.within(NC) and not (z.fixed and z.c >= NC - 2):
                    row_copy(z)
                if z.fixed and z.c >= NC - 1 and z.c <= NC:
                    row_copy(z + (-1))

            chunk(At(-3, -2, 1))
            act.wait_ge(s_cond, 16)
            act.activation(cond_th[:, :], cond_sb[:, :], ACT.Tanh, scale=0.5).then_inc(s_th, 1)
            act.wait_ge(s_setup_pe, 1)
            act.activation(condT[:, :], ps_k[:, 0:B], ACT.Copy, scale=0.5).then_inc(s_setup_act, 1)
            act.wait_ge(s_setup_pe, 7)
            act.activation(wT[:, :, :], ps_q[:, :].rearrange("p (n d) -> p n d", n=4), ACT.Copy).then_inc(s_setup_act, 1)
            walk(act, -2, *A_SPAN[1:], chunk)

            act.wait_ge(s_pads, 2)
            act.wait_ge(s_count, 1)
            write_pads(act, range(1, E, 2))
            act.wait_ge(s_sel, 1)
            act.activation(par[:, :, :], ps_x[:, 0:NV * NJ].rearrange("p (v j) -> p v j", v=NV),
                           ACT.Copy).then_inc(s_par, 1)
            act.wait_ge(s_par, 1)

            def column(v, j):
                return par[:, v, bass.ds(j, 1)]

            act.wait_ge(s_planned, 2)
            act.wait_ge(s_experts, 16 * (E // 2 + FC + 1))

            def expert_tile(j):
                n = j + 1
                if n.within(NJ):
                    e = expert_of(act, n)
                    wait(act, b_l1, FC * (n.c - 1))
                    act.activation(w1_sb[:, n.par, :], of_expert(w1_all, e, 0, F), ACT.Copy).then_inc(b_w1, 1)
                if j.within(NJ):
                    k = j.par
                    wait(act, b_y, j.c - 1)
                    for f, src in enumerate((ps_proj[:, 0:FT], ps_proj[:, FT:2 * FT], ps_h[:, 0:FT])):
                        if f != 1:
                            wait(act, b_l1, FC * j.c + (2, 2, 3)[f])
                        a = act.activation(hid[:, k, f, :], src, ACT.Relu, bias=column(2 + f, j.c))
                    a.then_inc(b_hidA, 1)
                if n.within(NJ):
                    wait(act, b_zTp, n.c + 1)
                    act.activation(zT[:, n.par, :], ps_z[:, 0:FT], ACT.Identity, bias=column(1, n.c),
                                   scale=column(0, n.c)).then_inc(b_zT, 1)

            walk(act, *B_SPAN, expert_tile, 4)

        @block.vector
        def _(dve):
            dve.memset(seq_mask[:, :], 1.0).then_inc(s_zero, 1)
            for k, (buf, v) in enumerate(((Kp, CUM_EPS), (KVp, 0.0))):
                dve.memset(buf[:, :, :, 0:1], v).then_inc(s_zero, 1)
            dve.memset(Ep[:, :, :, 0:2], 0.0).then_inc(s_zero, 1)
            dve.memset(Mp[:, :, :, 1:2], 0.0).then_inc(s_zero, 1)
            dve.wait_ge(s_zero, 1)
            dve.memset(seq_mask[:, :].rearrange("p (s l) -> p s l", s=CS)[:, :, 0:1], 0.0).then_inc(s_zero, 1)
            dve.memset(lnbias[:, :], LN_SHIFT).then_inc(s_lnb, 1)
            dve.memset(epsv[:, :], LN_EPS).then_inc(s_lnb, 1)

            def x_tile(at, t):
                return x_in[:, at.par, t, :]

            def x1_tile(at, t):
                return x1_all[:, bass.ds(at.c * CN + t, 1), :].rearrange("p o d -> p (o d)")

            def stats(at, s, src, kind):
                k = at.par if kind == 0 else 1 - at.par
                for t in range(CN):
                    dve.bn_stats(bn[kind][:, k, t, :], src(at, t)).then_inc(s["bn"], 1)

            def means(at, s, kind, tiles=range(CN)):
                k = at.par if kind == 0 else 1 - at.par
                if tiles[0] == 0:
                    wait(dve, s["norm"], CN * (at.c - 1))
                    wait(dve, s["bn"], CN * (at.c + 1))
                    alone(dve)
                for t in tiles:
                    dve.bn_aggr(mv[:, k, kind, t, :], bn[kind][:, k, t, :]).then_inc(s["aggr"], 1)

            def group_of(g, between):
                wait(dve, s_gates, 2 * (g + 1))
                lg = ps_gate[:, 0:GT * E].rearrange("p (t e) -> p t e", e=E)
                dve.tensor_reduce(top[:, :], lg, AX.X, ALU.max).then_inc(s_oh, 1)
                between(0)
                wait(dve, s_oh, 4 * g + 1)
                dve.tensor_tensor(is_top[:, :, :], lg, top[:, :].unsqueeze(2).to_broadcast([P, GT, E]),
                                  ALU.is_equal).then_inc(s_oh, 1)
                between(1)
                wait(dve, s_oh, 4 * g + 2)
                dve.tensor_tensor(is_top[:, :, :], is_top[:, :, :], expert_no[:, :, :], ALU.mult).then_inc(s_oh, 1)
                between(2)
                wait(dve, s_oh, 4 * g + 3)
                dve.tensor_reduce(pick[:, :], is_top[:, :, :], AX.X, ALU.min).then_inc(s_oh, 1)
                between(3)
                wait(dve, s_oh, 4 * g + 4)
                dve.scalar_tensor_tensor(out=onehot[:, :, :], in0=pick[:, :].unsqueeze(2).to_broadcast([P, GT, E]),
                                         scalar=-1.0, in1=expert_no[:, :, :], op0=ALU.min, op1=ALU.is_equal
                                         ).then_inc(s_ohr, 1)

            def slots_of(g, between):
                n = GT * E
                wait(dve, s_rank, g + 1)
                dve.tensor_copy(run_in[:, :, 0:1], run_out[:, :, GT:GT + 1]).then_inc(s_run, 1)
                dve.tensor_copy(run_in[:, :, 1:GT + 1],
                                ps_gate[:, 2 * n:3 * n].rearrange("p (e t) -> p e t", e=E)).then_inc(s_run, 1)
                between(0)
                wait(dve, s_run, 5 * g + 2)
                dve.tensor_tensor_scan(run_out[:, :, :].rearrange("p e t -> p (e t)"), run_mask[:, :],
                                       run_in[:, :, :].rearrange("p e t -> p (e t)"), 0.0, ALU.mult,
                                       ALU.add).then_inc(s_run, 1)
                between(1)
                wait(dve, s_run, 5 * g + 3)
                dve.tensor_tensor(slot_f[:, :, :], ps_gate[:, n:2 * n].rearrange("p (e t) -> p e t", e=E),
                                  run_out[:, :, 0:GT], ALU.add).then_inc(s_run, 1)
                between(2)
                wait(dve, s_run, 5 * g + 4)
                dve.tensor_tensor(slot_m[:, :, :], slot_f[:, :, :], onehot[:, :, :].rearrange("p t e -> p e t"),
                                  ALU.mult).then_inc(s_run, 1)
                between(3)
                wait(dve, s_run, 5 * g + 5)
                for k in range(2):
                    wait(dve, s_scat[k], 16 * CN * g)
                dve.tensor_reduce(slots[:, :], slot_m[:, :, :].rearrange("p e t -> p t e"), AX.X,
                                  ALU.add).then_inc(s_slot, 1)

            def chunk(c):
                here, k = c.within(NC), c.par
                q, s, a, o, y, r = c + 1, c + (-5), c + 4, c + (-1), c + (-2), c + (-3)
                if here:
                    wait(dve, s_SR, c.c + 1)
                    dve.scalar_tensor_tensor(out=Oar[:, k, :, 1:LP], in0=tq[:, k, :, 1:LP], scalar=1.0,
                                             in1=SRp[:, k, :, 1:LP], op0=ALU.add, op1=ALU.mult).then_inc(s_Oar, 1)
                    wait(dve, s_Oar, c.c + 1)
                    dve.scalar_tensor_tensor(out=Ep[:, k, :, 2:LP], in0=Oar[:, k, :, 1:L], scalar=-0.5,
                                             in1=hT[:, k, :, 2:LP], op0=ALU.mult, op1=ALU.add).then_inc(s_E, 1)
                if q.within(NC):
                    if q.fixed and q.c == 0:
                        dve.wait_ge(s_zero, 6)
                    wait(dve, s_K, q.c + 1)
                    dve.tensor_tensor_scan(Kc[:, q.par, :, :].rearrange("p s l -> p (s l)"), seq_mask[:, :],
                                           Kp[:, q.par, :, :].rearrange("p s l -> p (s l)"), 0.0,
                                           ALU.mult, ALU.add).then_inc(s_Kc, 1)
                w = c + 3

                def x_mean(t):
                    if w.within(NC):
                        means(w, sA, 0, [t])

                if s.par == 0 and s.within(NC):
                    slots_of(s.half, x_mean)
                else:
                    for t in range(CN):
                        x_mean(t)
                if here:
                    wait(dve, s_E, c.c + 1)
                    dve.scalar_tensor_tensor(out=Ep[:, k, :, 2:LP], in0=t2[:, k, :, 1:L], scalar=1.0,
                                             in1=Ep[:, k, :, 2:LP], op0=ALU.add, op1=ALU.mult).then_inc(s_KE, 1)
                if q.within(NC):
                    wait(dve, s_KV, q.c + 1)
                    dve.tensor_tensor_scan(Sc[:, q.par, :, :].rearrange("p s l -> p (s l)"), seq_mask[:, :],
                                           KVp[:, q.par, :, :].rearrange("p s l -> p (s l)"), 0.0,
                                           ALU.mult, ALU.add).then_inc(s_Sc, 1)
                if here:
                    wait(dve, s_KE, c.c + 1)
                    dve.tensor_tensor_scan(S2[:, k, :, :].rearrange("p s l -> p (s l)"), seq_mask[:, :],
                                           Ep[:, k, :, :].rearrange("p s l -> p (s l)"), 0.0,
                                           ALU.mult, ALU.add).then_inc(s_S2, 1)
                if a.within(NC):
                    wait(dve, s_x[a.par], 16 * (a.half + 1))
                    stats(a, sA, x_tile, 0)
                if here:
                    wait(dve, s_S2, c.c + 1)
                    dve.scalar_tensor_tensor(out=Mp[:, k, :, 2:LP], in0=tq[:, k, :, 1:L], scalar=1.0,
                                             in1=S2[:, k, :, 2:LP], op0=ALU.add, op1=ALU.mult).then_inc(s_M, 1)
                if o.within(NC):
                    wait(dve, s_proj, o.c + 1)
                    wait(dve, s_xr[o.par], 16 * (o.half + 1))
                    dve.tensor_tensor(x1_all[:, bass.ds(o.c * CN, CN), :], ps_proj[:, :].rearrange("p (t d) -> p t d", t=CN),
                                      x_res[:, o.par, :, :], ALU.add).then_inc(s_x1, 1)
                if here:
                    wait(dve, s_M, c.c + 1)
                    wait(dve, s_proj, c.c - 1)
                    dve.scalar_tensor_tensor(out=Ot[:, k, :, :], in0=Mp[:, k, :, 1:LP], scalar=0.5 * KAPPA,
                                             in1=Oar[:, k, :, 1:LP], op0=ALU.mult, op1=ALU.add).then_inc(s_O, 1)
                if o.within(NC):
                    wait(dve, s_x1, o.c + 1)
                    alone(dve)
                    stats(o, sB, x1_tile, 1)
                def normalise(t):
                    if y.within(NC):
                        if t == 0:
                            wait(dve, sB["aggr"], CN * (y.c + 1))
                            wait(dve, s_rstd, y.c + 6)
                            wait(dve, s_zT, y.c - 1)
                        dve.tensor_scalar(zz[:, y.par, t, :], x1_tile(y, t), mv[:, 1 - y.par, 1, t, 0:1],
                                          rstd[:, 1 - y.par, 1, t:t + 1], ALU.subtract, ALU.mult
                                          ).then_inc(sB["norm"], 1)

                if r.par == 1 and r.within(NC):
                    if r.fixed and r.c == 1:
                        dve.wait_ge(s_iota, 9 + 2 * E + 1)
                    group_of(r.half, normalise)
                else:
                    for t in range(CN):
                        normalise(t)
                if o.within(NC):
                    means(o, sB, 1)

            chunk(At(-4, -2, 0))
            chunk(At(-3, -2, 1))

            dve.wait_ge(s_th, 1)
            dve.scalar_tensor_tensor(out=cond_silu[:, :], in0=cond_th[:, :], scalar=1.0, in1=cond_sb[:, :],
                                     op0=ALU.add, op1=ALU.mult).then_inc(s_silu, 1)
            dve.wait_ge(s_setup_pe, 2)
            for n in range(4):
                dve.tensor_scalar(mod[:, n, :], ps_k2[:, n * B:(n + 1) * B], float(n % 2), None,
                                  ALU.add).then_inc(s_modw, 1)
            dve.wait_ge(s_modw, 4)
            dve.wait_ge(s_setup_pe, 3)
            g2 = ps_proj[0:B, 0:2 * D].rearrange("p (g d) -> p g d", g=2)
            dve.tensor_copy(gate_raw[:, :, :], g2).then_inc(s_gate, 1)
            chunk(At(-2, -1, 0))
            dve.wait_ge(s_gate, 1)
            dve.tensor_scalar(gate_sign[:, :, :], gate_raw[:, :, :], 0.0, 2.0, ALU.is_ge, ALU.mult).then_inc(s_gate, 1)
            dve.scalar_tensor_tensor(out=gate_abs[:, :, :], in0=gate_raw[:, :, :], scalar=-1.0,
                                     in1=gate_raw[:, :, :], op0=ALU.mult, op1=ALU.max).then_inc(s_gate, 1)
            dve.wait_ge(s_gate, 3)
            dve.tensor_scalar(gate_abs[:, :, :], gate_abs[:, :, :], 0.25, None, ALU.max).then_inc(s_gabs, 1)
            dve.wait_ge(s_gabs, 1)
            dve.scalar_tensor_tensor(out=gates[:, 0:2, :], in0=gate_sign[:, :, :], scalar=-1.0,
                                     in1=gate_abs[:, :, :], op0=ALU.add, op1=ALU.mult).then_inc(s_gate, 1)
            dve.wait_ge(s_gate, 4)
            dve.wait_ge(s_small, 16 * 4)
            dve.tensor_tensor(gates[:, 2, :], gates[:, 0, :], bproj_bc[:, :], ALU.mult).then_inc(s_gate, 1)
            dve.wait_ge(s_gate, 5)
            dve.tensor_scalar(gates[:, 0, :], gates[:, 0, :], 0.5, None, ALU.mult).then_inc(s_gate, 1)
            walk(dve, -1, *A_SPAN[1:], chunk)

            dve.wait_ge(s_slot, NT // GT)
            step = [0]

            def then(ins):
                step[0] += 1
                ins.then_inc(s_plan, 1)
                dve.wait_ge(s_plan, step[0])

            dve.tensor_copy(end_i[:, :], run_out[:, :, GT]).then_inc(s_count, 1)
            then(dve.tensor_tensor(count_f[:, :], run_out[:, :, GT], region[:, 0:E], ALU.subtract))
            then(dve.tensor_scalar(count_i[:, :], count_f[:, :], float(FT - 1), None, ALU.add))
            then(dve.tensor_scalar(tiles_i[:, :], count_i[:, :], FT.bit_length() - 1, None, ALU.arith_shift_right))
            then(dve.tensor_copy(tiles_f[:, :], tiles_i[:, :]))
            then(dve.tensor_tensor_scan(tiles_end[:, :], run_mask[:, 1:E + 1], tiles_f[:, :], 0.0, ALU.mult, ALU.add))
            then(dve.scalar_tensor_tensor(out=shift[:, 1:E + 1], in0=tiles_end[:, :], scalar=-float(FT),
                                          in1=region[:, 1:E + 1], op0=ALU.mult, op1=ALU.add))
            then(dve.memset(shift[:, 0:1], 0.0))
            then(dve.tensor_tensor(past[:, :, :], tile_no[:, :].unsqueeze(2).to_broadcast([P, NJ, E]),
                                   tiles_end[:, :].unsqueeze(1).to_broadcast([P, NJ, E]), ALU.is_ge))
            then(dve.tensor_reduce(tile_e[:, :], past[:, :, :], AX.X, ALU.add))
            then(dve.tensor_scalar(tile_ec[:, :], tile_e[:, :], float(E - 1), None, ALU.min))
            dve.tensor_scalar(sel[:, :], tile_ec[0:E, :], part_no[0:E, :], None, ALU.is_equal).then_inc(s_planned, 1)
            for e in range(E + 1):
                dve.tensor_scalar(is_e[:, :, e], tile_e[:, :], float(e), None, ALU.is_equal).then_inc(s_ise, 1)
            dve.wait_ge(s_ise, E + 1)
            then(dve.tensor_tensor(is_e[:, :, :], is_e[:, :, :],
                                   shift[:, :].unsqueeze(1).to_broadcast([P, NJ, E + 1]), ALU.mult))
            then(dve.tensor_reduce(row_f[:, :], is_e[:, :, :], AX.X, ALU.add))
            then(dve.scalar_tensor_tensor(out=row_g[:, :], in0=tile_no[:, :], scalar=float(FT), in1=row_f[:, :],
                                          op0=ALU.mult, op1=ALU.add))
            then(dve.tensor_copy(plan[:, :, 0], tile_ec[:, :]))
            dve.tensor_scalar(plan[:, :, 1], row_g[:, :], float(E * RS), None, ALU.min).then_inc(s_planned, 1)
            dve.wait_ge(s_par, 1)

            dve.wait_ge(s_experts, 16 * (E // 2 + FC + 1))

            def expert_tile(j):
                u, z, n = j + (-2), j + 2, j + 3
                if u.within(NJ):
                    e = expert_of(dve, u)
                if j.within(NJ):
                    k = j.par
                    wait(dve, b_l1, FC * (j.c + 1))
                    wait(dve, b_y, j.c - 1)
                    dve.tensor_scalar(hid[:, k, FC - 1, :], ps_k2[:, 0:FT],
                                      par[:, NV - 1, bass.ds(j.c, 1)], 0.0, ALU.add, ALU.max).then_inc(b_hidD, 1)
                if u.within(NJ):
                    wait(dve, b_y, u.c + 1)
                    wait(dve, s_uout[u.par], 16 * FS * u.half)
                    dve.tensor_tensor(u_sb[:, u.par, :, :],
                                      (ps_q, ps_k)[u.par][:, 0:FT].rearrange("p (s d) -> p s d", s=FS),
                                      b2_bc[:, bass.ds(e, 1), :].to_broadcast([P, FS, D]),
                                      ALU.add).then_inc(b_bias, 1)
                if z.within(NJ):
                    k = z.par
                    wait(dve, b_rstd, z.c + 1)
                    wait(dve, b_zTp, z.c - 1)
                    for t in range(FS):
                        dve.tensor_scalar(bz[:, k, t, :], rin[:, k, t, :], bmv[:, k, t, 0:1], brstd[:, k, t:t + 1],
                                          ALU.subtract, ALU.mult).then_inc(b_z, 1)
                def to_u(done, part, op, signal):
                    wait(dve, done, u.c + 1)
                    dve.tensor_tensor(u_sb[:, u.par, :, :], u_sb[:, u.par, :, :],
                                      full[:, u.par, :, part:part + D], op).then_inc(signal, 1)

                if u.within(NJ):
                    wait(dve, s_full[u.par], 16 * (u.half + 1))
                    to_u(b_bias, 0, ALU.add, b_sum)
                if n.within(NJ):
                    k = n.par
                    wait(dve, s_rin[k], 16 * (n.half + 1))
                    alone(dve)
                    for t in range(FS):
                        dve.bn_stats(bbn[:, k, t, :], rin[:, k, t, :]).then_inc(b_bn, 1)
                if u.within(NJ):
                    to_u(b_sum, W + D, ALU.mult, b_gated)
                if n.within(NJ):
                    wait(dve, b_bn, FS * (n.c + 1))
                    wait(dve, b_z, FS * (n.c - 1))
                    alone(dve)
                    for t in range(FS):
                        dve.bn_aggr(bmv[:, k, t, :], bbn[:, k, t, :]).then_inc(b_aggr, 1)
                if u.within(NJ):
                    to_u(b_gated, W, ALU.add, b_u)

            walk(dve, *B_SPAN, expert_tile, 4)


_INS = ['L0_attn_x', 'L0_attn_Wq1', 'L0_attn_bq1', 'L0_attn_Wk1', 'L0_attn_bk1', 'L0_attn_Wk2', 'L0_attn_bk2',
        'L0_attn_Wproj', 'L0_attn_bproj', 'L0_ffn_centroids', 'L0_ffn_ln_g', 'L0_ffn_ln_b', 'L0_ffn_W1',
        'L0_ffn_b1', 'L0_ffn_W2', 'L0_ffn_b2', 'L0_c', 'L0_wmod']
_OUTS = [((32, 256, 128), 'float32')]


def kernel(**inputs):
    import numpy as _np
    import concourse.bacc as _bacc
    from concourse import mybir as _mybir
    from concourse.bass_utils import run_bass_kernel_spmd as _run

    nc = _bacc.Bacc("TRN2", target_bir_lowering=False, num_devices=1)
    arrays, args = {}, []
    for name in _INS:
        a = _np.ascontiguousarray(inputs[name])
        arrays[f"in_{name}_dram"] = a
        args.append(nc.dram_tensor(f"in_{name}_dram", a.shape, _mybir.dt.from_np(a.dtype), kind="ExternalInput").ap())
    for i, (shape, dtype) in enumerate(_OUTS):
        dt = _mybir.dt.from_np(_np.dtype(dtype))
        args.append(nc.dram_tensor(f"out_{i}_dram", shape, dt, kind="ExternalOutput").ap())
    build_block(nc, *args)
    r = _run(nc, [arrays], core_ids=[0])
    got = tuple(r.results[0][f"out_{i}_dram"] for i in range(len(_OUTS)))
    return got[0]
```
